# Optimizing a Trainium2 kernel written in Bass

```python
import numpy as np
import jax
import jax.numpy as jnp

def _softmax(x, axis=-1):
    return jax.nn.softmax(x, axis=axis)

def _gelu(x):
    return jax.nn.gelu(x, approximate=True)

def _silu(x):
    return jax.nn.silu(x)

def _sigmoid(x):
    return jax.nn.sigmoid(x)

def _layernorm(x, axis=-1, eps=1e-05):
    m = jnp.mean(x, axis=axis, keepdims=True)
    v = jnp.var(x, axis=axis, keepdims=True)
    return (x - m) / jnp.sqrt(v + eps)

def _scatter_add(tgt, idx, src, axis=0):
    return tgt.at[idx].add(src)

def _segment_sum(src, seg, n):
    return jax.ops.segment_sum(src, seg, n)
kernel_name = 'mk_flamingo_gated_d2_seqx_r8_567ae5'

def setup_inputs(seed: int=0):
    np.random.seed(seed)
    _w = jnp.asarray

    def _rec_inputs():
        import jax
        import jax.numpy as jnp
        _rk = jax.random.key(seed)
        x = -0.0002928 + 1 * jax.random.normal(jax.random.fold_in(_rk, 1), (8, 256, 128), jnp.float32)
        _lenS = 256 - jax.random.randint(jax.random.fold_in(_rk, 7), (8,), 0, max(1, 256 // 4) + 1, jnp.int32)
        _lenS2 = 1601 - jax.random.randint(jax.random.fold_in(_rk, 8), (8,), 0, max(1, 1601 // 4) + 1, jnp.int32)
        _ctx_1024P = jax.random.normal(jax.random.fold_in(_rk, 11), (8, 16, 128), jnp.float32)
        _ctx_1024c = jax.random.dirichlet(jax.random.fold_in(_rk, 511), 0.3 * jnp.ones((16,), jnp.float32), (8, 1601))
        _ctx_1024t = jnp.einsum('bsk,bkd->bsd', _ctx_1024c, _ctx_1024P)
        _ctx_1024t = _ctx_1024t * jax.lax.rsqrt(jnp.mean(jnp.square(_ctx_1024t)) + 1e-12) * 0.953939
        ctx_1024 = -1.39393e-06 + 0.999914 * (_ctx_1024t + 0.3 * jax.random.normal(jax.random.fold_in(_rk, 611), (8, 1601, 128), jnp.float32))
        fside_BxSxS2_0 = -1.47943e-05 + 1.00017 * jax.random.normal(jax.random.fold_in(_rk, 12), (8, 256, 1601), jnp.float32)
        _g = jax.random.normal(jax.random.fold_in(_rk, 9001), (2, 2), jnp.float32)
        _g = jnp.sign(_g) * jnp.maximum(jnp.abs(_g), 1.0) + (_g == 0) * 1.0
        g_xattn = _g[0]
        g_ffn = _g[1]
        return (x, ctx_1024, fside_BxSxS2_0, g_xattn, g_ffn)
    x, ctx_1024, fside_BxSxS2_0, g_xattn, g_ffn = _rec_inputs()

    def _L0_xattn_setup():
        import math
        import jax, jax.numpy as jnp
        import numpy as np
        EMBED = 128
        INTERNAL = 128
        HEADS = 16

        def _split_heads(x):
            b, n, c = x.shape
            return x.reshape(b, n, HEADS, c // HEADS).transpose(0, 2, 1, 3)
        key = jax.random.key(seed)
        ks = jax.random.split(key, 11)
        b, n, m = (2, 256, 256)
        s = 1.0 / math.sqrt(EMBED)
        inp = {'q': jax.random.normal(ks[0], (b, n, EMBED), jnp.float32), 'k': jax.random.normal(ks[1], (b, m, EMBED), jnp.float32), 'v': jax.random.normal(ks[2], (b, m, EMBED), jnp.float32), 'Wq': jax.random.normal(ks[3], (EMBED, INTERNAL), jnp.float32) * s, 'bq': jax.random.normal(ks[4], (INTERNAL,), jnp.float32) * s, 'Wk': jax.random.normal(ks[5], (EMBED, INTERNAL), jnp.float32) * s, 'bk': jax.random.normal(ks[6], (INTERNAL,), jnp.float32) * s, 'Wv': jax.random.normal(ks[7], (EMBED, INTERNAL), jnp.float32) * s, 'bv': jax.random.normal(ks[8], (INTERNAL,), jnp.float32) * s, 'Wo': jax.random.normal(ks[9], (INTERNAL, EMBED), jnp.float32) * s, 'bo': jax.random.normal(ks[10], (EMBED,), jnp.float32) * s}
        return inp
    _L0_xattn_all = _L0_xattn_setup()
    _L0_xattn_in = {k: v for k, v in _L0_xattn_all.items() if k in ('Wq', 'bq', 'Wk', 'bk', 'Wv', 'bv', 'Wo', 'bo')}
    del _L0_xattn_all

    def _L0_ffn_setup():
        import jax, jax.numpy as jnp
        import numpy as np
        EMB, HID, E, TOPK = (128, 512, 8, 2)
        key = jax.random.key(seed)
        ks = jax.random.split(key, 10)
        s = 0.02
        return {'x': jax.random.normal(ks[0], (4, 256, EMB), jnp.float32), 'rw1': s * jax.random.normal(ks[1], (EMB, HID), jnp.float32), 'rb1': jnp.zeros((HID,), jnp.float32), 'rw2': s * jax.random.normal(ks[2], (HID, E), jnp.float32), 'rb2': jnp.zeros((E,), jnp.float32), 'w1': s * jax.random.normal(ks[3], (E, EMB, HID), jnp.float32), 'b1': jnp.zeros((E, HID), jnp.float32), 'w2': s * jax.random.normal(ks[4], (E, HID, EMB), jnp.float32), 'b2': jnp.zeros((E, EMB), jnp.float32)}
    _L0_ffn_all = _L0_ffn_setup()
    _L0_ffn_in = {k: v for k, v in _L0_ffn_all.items() if k in ('rw1', 'rb1', 'rw2', 'rb2', 'w1', 'b1', 'w2', 'b2')}
    del _L0_ffn_all

    def _L1_xattn_setup():
        import jax, jax.numpy as jnp
        import numpy as np
        D = 128
        key = jax.random.key(seed)
        ks = jax.random.split(key, 13)
        B, S, d = (4, 256, D)
        inp = {'q_in': jax.random.normal(ks[0], (B, S, d), jnp.float32), 'k_in': jax.random.normal(ks[1], (B, S, d), jnp.float32), 'v_in': jax.random.normal(ks[2], (B, S, d), jnp.float32), 'phi_risk': jax.random.normal(ks[3], (B, S, S), jnp.float32), 'phi_prio': jax.random.normal(ks[4], (B, S, S), jnp.float32), 'phi_impl': jax.random.normal(ks[5], (B, S, S), jnp.float32), 'Wq': jax.random.normal(ks[6], (d, d), jnp.float32) / np.sqrt(d), 'bq': jax.random.normal(ks[7], (d,), jnp.float32) * 0.01, 'Wk': jax.random.normal(ks[8], (d, d), jnp.float32) / np.sqrt(d), 'bk': jax.random.normal(ks[9], (d,), jnp.float32) * 0.01, 'Wv': jax.random.normal(ks[10], (d, d), jnp.float32) / np.sqrt(d), 'bv': jax.random.normal(ks[11], (d,), jnp.float32) * 0.01, 'beta_risk': jnp.float32(0.1), 'beta_prio': jnp.float32(0.1), 'beta_impl': jnp.float32(0.1)}
        return inp
    _L1_xattn_all = _L1_xattn_setup()
    _L1_xattn_in = {k: v for k, v in _L1_xattn_all.items() if k in ('Wq', 'bq', 'Wk', 'bk', 'Wv', 'bv', 'beta_risk', 'beta_prio', 'beta_impl')}
    del _L1_xattn_all

    def _L1_ffn_setup():
        import jax, jax.numpy as jnp
        import numpy as np
        D_MODEL = 128
        N_EXPERTS = 8
        TOP_K = 2
        FFN_HIDDEN = 4 * D_MODEL
        key = jax.random.key(seed)
        ks = jax.random.split(key, 6)

        def xavier(k, shape):
            fan_in, fan_out = (shape[-2], shape[-1])
            lim = jnp.sqrt(6.0 / (fan_in + fan_out))
            return jax.random.uniform(k, shape, jnp.float32, -lim, lim)
        x = jax.random.normal(ks[0], (4, 256, D_MODEL), jnp.float32)
        w_gate = xavier(ks[1], (N_EXPERTS, D_MODEL))
        W1 = xavier(ks[2], (N_EXPERTS, D_MODEL, FFN_HIDDEN))
        b1 = jnp.zeros((N_EXPERTS, FFN_HIDDEN), jnp.float32)
        W2 = xavier(ks[3], (N_EXPERTS, FFN_HIDDEN, D_MODEL))
        b2 = jnp.zeros((N_EXPERTS, D_MODEL), jnp.float32)
        return {'x': x, 'w_gate': w_gate, 'W1': W1, 'b1': b1, 'W2': W2, 'b2': b2}
    _L1_ffn_all = _L1_ffn_setup()
    _L1_ffn_in = {k: v for k, v in _L1_ffn_all.items() if k in ('w_gate', 'W1', 'b1', 'W2', 'b2')}
    del _L1_ffn_all
    return {'x': x, 'ctx_1024': ctx_1024, 'fside_BxSxS2_0': fside_BxSxS2_0, 'g_xattn': g_xattn, 'g_ffn': g_ffn, 'L0_xattn_Wq': _L0_xattn_in['Wq'], 'L0_xattn_bq': _L0_xattn_in['bq'], 'L0_xattn_Wk': _L0_xattn_in['Wk'], 'L0_xattn_bk': _L0_xattn_in['bk'], 'L0_xattn_Wv': _L0_xattn_in['Wv'], 'L0_xattn_bv': _L0_xattn_in['bv'], 'L0_xattn_Wo': _L0_xattn_in['Wo'], 'L0_xattn_bo': _L0_xattn_in['bo'], 'L0_ffn_rw1': _L0_ffn_in['rw1'], 'L0_ffn_rb1': _L0_ffn_in['rb1'], 'L0_ffn_rw2': _L0_ffn_in['rw2'], 'L0_ffn_rb2': _L0_ffn_in['rb2'], 'L0_ffn_w1': _L0_ffn_in['w1'], 'L0_ffn_b1': _L0_ffn_in['b1'], 'L0_ffn_w2': _L0_ffn_in['w2'], 'L0_ffn_b2': _L0_ffn_in['b2'], 'L1_xattn_Wq': _L1_xattn_in['Wq'], 'L1_xattn_bq': _L1_xattn_in['bq'], 'L1_xattn_Wk': _L1_xattn_in['Wk'], 'L1_xattn_bk': _L1_xattn_in['bk'], 'L1_xattn_Wv': _L1_xattn_in['Wv'], 'L1_xattn_bv': _L1_xattn_in['bv'], 'L1_xattn_beta_risk': _L1_xattn_in['beta_risk'], 'L1_xattn_beta_prio': _L1_xattn_in['beta_prio'], 'L1_xattn_beta_impl': _L1_xattn_in['beta_impl'], 'L1_ffn_w_gate': _L1_ffn_in['w_gate'], 'L1_ffn_W1': _L1_ffn_in['W1'], 'L1_ffn_b1': _L1_ffn_in['b1'], 'L1_ffn_W2': _L1_ffn_in['W2'], 'L1_ffn_b2': _L1_ffn_in['b2']}

def reference(x, ctx_1024, fside_BxSxS2_0, g_xattn, g_ffn, L0_xattn_Wq, L0_xattn_bq, L0_xattn_Wk, L0_xattn_bk, L0_xattn_Wv, L0_xattn_bv, L0_xattn_Wo, L0_xattn_bo, L0_ffn_rw1, L0_ffn_rb1, L0_ffn_rw2, L0_ffn_rb2, L0_ffn_w1, L0_ffn_b1, L0_ffn_w2, L0_ffn_b2, L1_xattn_Wq, L1_xattn_bq, L1_xattn_Wk, L1_xattn_bk, L1_xattn_Wv, L1_xattn_bv, L1_xattn_beta_risk, L1_xattn_beta_prio, L1_xattn_beta_impl, L1_ffn_w_gate, L1_ffn_W1, L1_ffn_b1, L1_ffn_W2, L1_ffn_b2):
    import jax
    import jax.numpy as jnp

    def _L0_xattn_ref(q, k, v, Wq, bq, Wk, bk, Wv, bv, Wo, bo):
        import math
        import jax, jax.numpy as jnp
        import numpy as np
        EMBED = 128
        INTERNAL = 128
        HEADS = 16

        def _split_heads(x):
            b, n, c = x.shape
            return x.reshape(b, n, HEADS, c // HEADS).transpose(0, 2, 1, 3)
        qh = _split_heads(q @ Wq + bq)
        kh = _split_heads(k @ Wk + bk)
        vh = _split_heads(v @ Wv + bv)
        c_per_head = kh.shape[-1]
        attn = jnp.einsum('bhnc,bhmc->bhnm', qh, kh) / math.sqrt(c_per_head)
        attn = jax.nn.softmax(attn, axis=-1)
        out = jnp.einsum('bhnm,bhmc->bhnc', attn, vh)
        b, h, n, ch = out.shape
        out = out.transpose(0, 2, 1, 3).reshape(b, n, h * ch)
        return out @ Wo + bo

    def _L0_ffn_ref(x, rw1, rb1, rw2, rb2, w1, b1, w2, b2):
        import jax, jax.numpy as jnp
        import numpy as np
        EMB, HID, E, TOPK = (128, 512, 8, 2)
        B, S, D = x.shape
        logits = jax.nn.silu(jnp.einsum('bsd,dh->bsh', x, rw1) + rb1)
        logits = jnp.einsum('bsh,he->bse', logits, rw2) + rb2
        k_logits, k_index = jax.lax.top_k(logits, TOPK)
        k_prob = jax.nn.softmax(k_logits, axis=-1)
        xf = x.reshape(B * S, D)
        k_index_f = k_index.reshape(B * S, TOPK)
        k_prob_f = k_prob.reshape(B * S, TOPK)
        out = jnp.zeros_like(xf)
        for e in range(E):
            we = jnp.sum(jnp.where(k_index_f == e, k_prob_f, 0.0), axis=-1)
            h = jax.nn.silu(xf @ w1[e] + b1[e]) @ w2[e] + b2[e]
            out = out + we[:, None] * h
        return out.reshape(B, S, D)

    def _L1_xattn_ref(q_in, k_in, v_in, phi_risk, phi_prio, phi_impl, Wq, bq, Wk, bk, Wv, bv, beta_risk, beta_prio, beta_impl):
        import jax, jax.numpy as jnp
        import numpy as np
        D = 128
        d = q_in.shape[-1]
        scale = jnp.asarray(d, q_in.dtype) ** (-0.5)
        Q = q_in @ Wq.T + bq
        K = k_in @ Wk.T + bk
        V = v_in @ Wv.T + bv
        att = jnp.einsum('bsd,btd->bst', Q, K) * scale
        att = att + beta_risk * phi_risk + beta_prio * phi_prio - beta_impl * phi_impl
        w = jax.nn.softmax(att, axis=-1)
        return jnp.einsum('bst,btd->bsd', w, V)

    def _L1_ffn_ref(x, w_gate, W1, b1, W2, b2):
        import jax, jax.numpy as jnp
        import numpy as np
        D_MODEL = 128
        N_EXPERTS = 8
        TOP_K = 2
        FFN_HIDDEN = 4 * D_MODEL
        B, S, D = x.shape
        flat_x = x.reshape(-1, D)
        gate = jax.nn.softmax(flat_x @ w_gate.T, axis=-1)
        topk_scores, topk_idx = jax.lax.top_k(gate, TOP_K)
        cw = (jax.nn.one_hot(topk_idx, N_EXPERTS, dtype=flat_x.dtype) * topk_scores[..., None]).sum(axis=1)
        h = jax.nn.gelu(jnp.einsum('td,edh->teh', flat_x, W1) + b1, approximate=False)
        y = jnp.einsum('teh,ehd->ted', h, W2) + b2
        out = jnp.einsum('ted,te->td', y, cw)
        return out.reshape(B, S, D)
    x = x + jnp.tanh(g_xattn[0]) * _L0_xattn_ref(_layernorm(x, axis=-1), ctx_1024, ctx_1024, L0_xattn_Wq, L0_xattn_bq, L0_xattn_Wk, L0_xattn_bk, L0_xattn_Wv, L0_xattn_bv, L0_xattn_Wo, L0_xattn_bo)
    x = x + jnp.tanh(g_ffn[0]) * _L0_ffn_ref(_layernorm(x, axis=-1), L0_ffn_rw1, L0_ffn_rb1, L0_ffn_rw2, L0_ffn_rb2, L0_ffn_w1, L0_ffn_b1, L0_ffn_w2, L0_ffn_b2)
    x = x + jnp.tanh(g_xattn[1]) * _L1_xattn_ref(_layernorm(x, axis=-1), ctx_1024, ctx_1024, fside_BxSxS2_0, fside_BxSxS2_0, fside_BxSxS2_0, L1_xattn_Wq, L1_xattn_bq, L1_xattn_Wk, L1_xattn_bk, L1_xattn_Wv, L1_xattn_bv, L1_xattn_beta_risk, L1_xattn_beta_prio, L1_xattn_beta_impl)
    x = x + jnp.tanh(g_ffn[1]) * _L1_ffn_ref(_layernorm(x, axis=-1), L1_ffn_w_gate, L1_ffn_W1, L1_ffn_b1, L1_ffn_W2, L1_ffn_b2)
    return x

_drawn_inputs = setup_inputs


def setup_inputs(seed=0):
    import zlib

    import numpy as np

    out = dict(_drawn_inputs(seed))
    spreads = {'g_ffn': (-1.0, 0.6),
     'L0_ffn_rb1': (0.0, 0.345),
     'L0_ffn_rb2': (0.0, 0.1),
     'L0_ffn_b1': (0.0, 0.486),
     'L0_ffn_b2': (0.0, 0.1),
     'L1_ffn_b1': (0.0, 0.1),
     'L1_ffn_b2': (0.0, 0.1)}
    factors = {'fside_BxSxS2_0': 8.0,
     'L0_xattn_bq': 3.318,
     'L0_xattn_bk': 64.0,
     'L1_xattn_bq': 21.811,
     'L1_xattn_bk': 64.0,
     'L1_xattn_bv': 5.292}
    for name, (base, spread) in spreads.items():
        noise = np.random.default_rng([zlib.crc32(name.encode()), seed]).standard_normal(out[name].shape)
        drawn = base * np.exp(spread * noise) if base else spread * noise
        out[name] = jnp.asarray(drawn.astype(out[name].dtype))
    for name, factor in factors.items():
        out[name] = (out[name] * factor).astype(out[name].dtype)
    return out
```

```python
import concourse.bass as bass
from concourse import mybir
from contextlib import ExitStack

BATCH, SEQ, CTX, DIM = 8, 256, 1601, 128
HEADS, HD = 16, 8
EXPERTS, HID = 8, 512
PART = 128
QT = SEQ // PART
KT = -(-CTX // PART)
HC = HID // PART
PAIRS = BATCH // 2
BANK = 512
CHUNKS = [(c, min(BANK, CTX - c)) for c in range(0, CTX, BANK)]
GH = 4
GROUPS = HEADS // GH
NG = 2 * GROUPS
ROWS = PART // GH
MAX_SCALE = 64.0
STAGES = 4
EPS = 1e-5


def tile_rows(t):
    return min(PART, CTX - t * PART)


def attention_events(i, t):
    ev = []
    if 1 <= t <= 8 and i + 1 < NG:
        ev.append(("s1", i + 1, t - 1))
    if t == 3 and i > 0:
        ev.append(("ot", i - 1, 0))
    if t == 5 and i == GROUPS:
        ev.append(("at", 0, 0))
    if t == 7 and i == GROUPS:
        ev.append(("op", 0, 0))
    if t == 10 and i + 1 < NG:
        ev.append(("mw", i + 1, 0))
    return ev


A_PREP = len(CHUNKS) + -(-KT // 2) + 2
A_ATTN0 = NG * (8 * len(CHUNKS) + 2) + 2 * 2
A_MOE = 1 + EXPERTS + 2
A_ATTN1 = 1 + QT * (2 * len(CHUNKS) + 1)
A_BODY = A_ATTN0 + 2 * (3 + 2 * A_MOE + A_ATTN1 + A_PREP)
A_LAST = A_BODY - 2 * A_PREP
PREP_AT = (A_BODY - 2 * A_PREP - (1 + A_MOE), A_BODY - A_PREP)
B_PREP = 2
C_NORM = 6
C_PREP = len(CHUNKS) + C_NORM + 1
C_BODY = 3 * NG + 2 * (1 + C_NORM) + 4 * C_NORM + 2 * (QT * 2) + 2 * 6 + 2 * 6 + 2 * C_PREP
B_BODY = NG * KT + 2 * (2 * EXPERTS + 1 + B_PREP)


class Ring:

    def __init__(self, base, depth):
        self.base, self.depth, self.n = base, depth, 0

    def next(self):
        self.n += 1
        return (self.n - 1) % self.depth

    def done(self):
        return self.base + self.n

    def reusable(self):
        return self.base + max(self.n - self.depth, 0)


def flamingo(nc, io, out):
    fp32, fp16, u32 = mybir.dt.float32, mybir.dt.float16, mybir.dt.uint32
    ALU, ACT, AX = mybir.AluOpType, mybir.ActivationFunctionType, mybir.AxisListType
    ctx = ExitStack()
    with ctx:
        def sb(name, shape, dt=fp32):
            return ctx.enter_context(nc.sbuf_tensor(name, shape, dt))

        def sem(name):
            return ctx.enter_context(nc.semaphore(name))

        ident = sb("ident", [PART, PART])
        iota = sb("iota", [PART, EXPERTS])
        wk0, wq0, wo0, wk1, wq1 = (sb(n, [DIM, DIM]) for n in ("wk0", "wq0", "wo0", "wk1", "wq1"))
        wv = sb("wv", [DIM, 2 * DIM])
        rw1, rw2, wg = sb("rw1", [DIM, HID]), sb("rw2", [PART, HC, EXPERTS]), sb("wg", [DIM, EXPERTS])
        w1 = [sb(f"w1_{l}", [DIM, EXPERTS, HID]) for l in range(2)]
        w2 = [sb(f"w2_{l}", [PART, EXPERTS, HC, DIM]) for l in range(2)]
        b1 = [sb(f"b1_{l}", [PART, EXPERTS, HC]) for l in range(2)]
        b2 = [sb(f"b2_{l}", [EXPERTS, DIM]) for l in range(2)]
        bcol = sb("bcol", [PART, 4])
        rb1 = sb("rb1", [PART, HC])
        bv = sb("bv", [PART, 2 * DIM])
        bo = sb("bo", [PART, DIM])
        rb2 = sb("rb2", [PART, EXPERTS])
        gates = sb("gates", [PART, 4])
        tgate = sb("tgate", [PART, 4])
        betas = sb("betas", [PART, 4])
        neghalf = sb("neghalf", [PART, QT])

        xres = [sb(f"xres{s}", [PART, QT, DIM]) for s in range(2)]
        xout = [sb(f"xout{s}", [PART, QT, DIM]) for s in range(2)]
        y = [sb(f"y{s}", [PART, QT, DIM]) for s in range(2)]
        yT = [sb(f"yT{s}", [DIM, SEQ]) for s in range(2)]
        vst = [sb(f"vst{s}", [PART, KT, HEADS, HD + 1]) for s in range(2)]
        k1T = [sb(f"k1T{s}", [DIM, CTX]) for s in range(2)]
        v1 = [sb(f"v1_{s}", [PART, KT, DIM]) for s in range(2)]
        ctxT = sb("ctxT", [DIM, CTX])
        khi, klo = sb("khi", [DIM, CTX], fp16), sb("klo", [DIM, CTX], fp16)
        qhi, qlo = sb("qhi", [DIM, SEQ], fp16), sb("qlo", [DIM, SEQ], fp16)
        kst = [sb(f"kst{r}", [PART, CTX], fp16) for r in range(STAGES)]
        qst = [sb(f"qst{r}", [PART, GH, 2, SEQ], fp16) for r in range(STAGES)]
        probs = [sb(f"probs{r}", [PART, GH * SEQ]) for r in range(2)]
        mxp = sb("mxp", [PART, 2 * GH, len(CHUNKS)])
        mw = sb("mw", [PART, QT, PART])
        m16 = sb("m16", [PART, GH, QT], fp16)
        oTs = sb("oTs", [PART, SEQ])
        rec = sb("rec", [PART, QT, GH])
        attn = sb("attn", [PART, QT, DIM])
        attnT = sb("attnT", [DIM, SEQ])
        oproj = sb("oproj", [PART, QT, DIM])
        hid = [sb(f"hid{r}", [PART, HC, SEQ]) for r in range(2)]
        acc = sb("acc", [PART, QT, DIM])
        q1T = sb("q1T", [DIM, SEQ])
        sc1 = [sb(f"sc1_{r}", [PART, CTX]) for r in range(QT)]
        p1T = sb("p1T", [PART, KT, PART])
        mx1 = sb("mx1", [PART, QT, len(CHUNKS)])
        nm1, sum1, rs1 = (sb(n, [PART, QT]) for n in ("nm1", "sum1", "rs1"))
        bst = sb("bst", [PART, QT, 6])
        mv = sb("mv", [PART, QT, 2])
        vpe, rst, nt1, nt2 = (sb(n, [PART, QT]) for n in ("vpe", "rst", "nt1", "nt2"))
        rr = sb("rr", [PART, QT])
        lg = sb("lg", [PART, QT, EXPERTS])
        eg = sb("eg", [PART, QT, EXPERTS])
        m8 = sb("m8", [PART, QT, 8])
        i8 = sb("i8", [PART, QT, 8], u32)
        i8f = sb("i8f", [PART, QT, 2])
        dm, tm, pr = sb("dm", [PART, QT]), sb("tm", [PART, QT]), sb("pr", [PART, QT, 2])
        nmg, sumg, rg = (sb(n, [PART, QT]) for n in ("nmg", "sumg", "rg"))
        oh = sb("oh", [PART, QT, 2, EXPERTS])
        we = sb("we", [PART, QT, EXPERTS])
        weT = sb("weT", [EXPERTS, QT, PART])

        pA = [ctx.enter_context(nc.psum_tensor(f"pA{i}", [PART, BANK], fp32)) for i in range(3)]
        pB = [ctx.enter_context(nc.psum_tensor(f"pB{i}", [PART, 2 * BANK], fp32)) for i in range(2)]
        pO = ctx.enter_context(nc.psum_tensor("pO", [PART, BANK], fp32))

        kscr = [nc.dram_tensor(f"kscr{s}", (HEADS, 4, HD, CTX), fp16, kind="Internal").ap() for s in range(2)]
        qscr = [nc.dram_tensor(f"qscr{s}", (HEADS, 4, HD, SEQ), fp16, kind="Internal").ap() for s in range(2)]

        w_in = sem("w_in")
        we_in = sem("we_in")
        pad_in = sem("pad_in")
        zeroed = sem("zeroed")
        x_in = [sem(f"x_in{s}") for s in range(2)]
        ctx_in = sem("ctx_in")
        side_in = [sem(f"side_in{r}") for r in range(QT)]
        stage_in = [sem(f"stage_in{r}") for r in range(STAGES)]
        k_stored = sem("k_stored")
        q_stored = sem("q_stored")
        out_stored = [sem(f"out_stored{s}") for s in range(2)]
        a_full, a_done = sem("a_full"), sem("a_done")
        b_full, b_done = sem("b_full"), sem("b_done")
        pv_full, pv_done = sem("pv_full"), sem("pv_done")
        y_ready = sem("y_ready")
        var_ready, rstd_ready = sem("var_ready"), sem("rstd_ready")
        mw_ready = sem("mw_ready")
        side_scaled = sem("side_scaled")
        coef_ready = sem("coef_ready")
        nm1_ready, p1_ready = sem("nm1_ready"), sem("p1_ready")
        dm_ready, tm_ready = sem("dm_ready"), sem("tm_ready")
        nmg_ready, eg_ready = sem("nmg_ready"), sem("eg_ready")
        we_ready = sem("we_ready")
        x_final = sem("x_final")
        tgate_ready = sem("tgate_ready")
        chain = sem("chain")

        passed, pool_passed = sem("passed"), sem("pool_passed")

        block = ctx.enter_context(nc.Block())

        x_v = io["x"].rearrange("(j s) (q p) d -> j s p q d", s=2, p=PART)
        out_v = out.rearrange("(j s) (q p) d -> j s p q d", s=2, p=PART)
        ctx_v = io["ctxT"].rearrange("(j s) d t -> j s d t", s=2)
        side_v = io["side"].rearrange("(j s) (q p) t -> j s q p t", s=2, p=PART)

        def at(view, it, *rest):
            if isinstance(it, int):
                return view[(it, *rest)]
            v = view[bass.ds(it, 1)]
            return v[(0, *rest)]

        @block.sync
        def _(sp):
            def load(dst, src, s):
                sp.dma_start(dst, src).then_inc(s, 16)

            def load_x(j, s):
                load(xres[s][:, :, :], at(x_v, j, s), x_in[s])

            def load_ctx(j, s):
                load(ctxT[:, :], at(ctx_v, j, s), ctx_in)

            def store_k(s, kn):
                sp.wait_ge(a_done, kn)
                for p, src in ((1, khi), (2, klo), (3, khi)):
                    sp.dma_start(kscr[s][:, p, :, :], src[:, :]).then_inc(k_stored, 16)

            def store_q(s, qn):
                sp.wait_ge(a_done, qn)
                for p, src in ((1, qhi), (2, qhi), (3, qlo)):
                    sp.dma_start(qscr[s][:, p, :, :], src[:, :]).then_inc(q_stored, 16)

            def stage(i, j):
                s, g, r = i // GROUPS, i % GROUPS, i % STAGES
                if g == 0:
                    sp.wait_ge(k_stored, 48 * (2 * j + s + 1))
                    sp.wait_ge(q_stored, 48 * (2 * j + s + 1))
                if i >= STAGES:
                    sp.wait_ge(b_full, 2 * B_PREP + B_BODY * j + (i - STAGES + 1) * KT)
                hs = slice(g * GH, (g + 1) * GH)
                sp.dma_start(kst[r][:, :], kscr[s][hs].rearrange("h p c t -> (h p c) t")).then_inc(stage_in[r], 16)
                for h in range(GH):
                    src = qscr[s][g * GH + h].rearrange("p c q -> (p c) q")
                    for v in range(2):
                        sp.dma_start(qst[r][ROWS * h:ROWS * (h + 1), h, v, :], src).then_inc(stage_in[r], 16)

            early = [(ident, "ident"), (iota, "iota"), (wk0, "wk0"), (wq0, "wq0"), (wo0, "wo0"), (wk1, "wk1"),
                     (wq1, "wq1"), (wv, "wv"), (bcol, "bcol"), (bv, "bv"), (bo, "bo"), (gates, "gates"),
                     (betas, "betas"), (rb1, "rb1"), (rb2, "rb2"), (rw1, "rw1"), (wg, "wg")]
            for s in range(2):
                sp.sem_inc(out_stored[s], 16)
            load_ctx(0, 0)
            load_x(0, 0)
            load_x(0, 1)
            for dst, name in early:
                d = dst[:, 0:3] if name == "betas" else dst[:, :]
                load(d, io[name], w_in)
            load(rw2[:, :, :], io["rw2"], w_in)
            for s in range(2):
                sp.dma_start(kscr[s][:, 0, :, :], io["kpad"]).then_inc(pad_in, 16)
                sp.dma_start(qscr[s][:, 0, :, :], io["qpad"]).then_inc(pad_in, 16)
            sp.wait_ge(pad_in, 64)
            sp.wait_ge(zeroed, 2)
            sp.wait_ge(a_full, A_PREP - 2)
            load_ctx(0, 1)
            store_k(0, len(CHUNKS))
            store_q(0, A_PREP)
            for i in range(STAGES):
                stage(i, 0)
            for l in range(2):
                load(w1[l][:, :, :], io[f"w1_{l}"], we_in)
                load(w2[l][:, :, :, :], io[f"w2_{l}"], we_in)
                load(b1[l][:, :, :], io[f"b1_{l}"], we_in)
                load(b2[l][:, :], io[f"b2_{l}"], we_in)
            store_k(1, A_PREP + len(CHUNKS))
            store_q(1, 2 * A_PREP)

            def body(j, last):
                for r in range(QT):
                    if not isinstance(j, int) or j > 0:
                        sp.wait_ge(a_full, 2 * A_PREP + A_BODY * j)
                    load(sc1[r][:, :], at(side_v, j, 0, r), side_in[r])
                for i in range(STAGES, NG):
                    stage(i, j)
                base = 2 * A_PREP + A_BODY * j
                yt = base + A_ATTN0 + 2 * (1 + A_MOE)
                for r in range(QT):
                    sp.wait_ge(a_full, yt + 2 + QT * len(CHUNKS) + (r + 1) * len(CHUNKS) + r)
                    load(sc1[r][:, :], at(side_v, j, 1, r), side_in[r])
                for s in range(2):
                    if not last:
                        sp.wait_ge(a_full, base if s == 0 else base + PREP_AT[0] + A_PREP - 2)
                        load_ctx(j + 1, s)
                    sp.wait_ge(x_final, 2 * j + s + 1)
                    sp.dma_start(at(out_v, j, s), xout[s][:, :, :]).then_inc(out_stored[s], 16)
                    if not last:
                        load_x(j + 1, s)
                        store_k(s, base + PREP_AT[s] + len(CHUNKS))
                        store_q(s, base + PREP_AT[s] + A_PREP)
                        if s == 0:
                            for i in range(STAGES):
                                stage(i, j + 1)

            with sp.Fori(0, PAIRS - 1) as j:
                body(j, False)
            body(PAIRS - 1, True)
            for s in range(2):
                sp.wait_ge(out_stored[s], 16 * (PAIRS + 1))

        @block.gpsimd
        def _(pool):
            pool.memset(neghalf[:, :], -0.5).then_inc(zeroed, 1)
            pool.wait_ge(zeroed, 1)

            def rstd(n):
                pool.wait_ge(var_ready, n)
                pool.tensor_tensor(rst[:, :], vpe[:, :], neghalf[:, :], ALU.pow).then_inc(rstd_ready, 1)

            def scale_side(r, m, n):
                pool.wait_ge(side_in[r], m)
                pool.sem_inc(pool_passed, 1)
                pool.tensor_scalar(sc1[r][:, :], sc1[r][:, :], betas[:, 3:4], 0.0, ALU.mult, ALU.add)\
                    .then_inc(side_scaled, 1)

            rstd(1)
            rstd(2)
            pool.wait_ge(coef_ready, 1)

            def body(j, last):
                base = 2 + 8 * j
                rstd(base + 1)
                rstd(base + 2)
                for r in range(QT):
                    scale_side(r, 16 * (2 * j + 1), 4 * j + r + 1)
                rstd(base + 3)
                rstd(base + 4)
                for r in range(QT):
                    scale_side(r, 16 * (2 * j + 2), 4 * j + 2 + r + 1)
                rstd(base + 5)
                rstd(base + 6)
                if not last:
                    rstd(base + 7)
                    rstd(base + 8)

            with pool.Fori(0, PAIRS - 1) as j:
                body(j, False)
            body(PAIRS - 1, True)

        @block.scalar
        def _(act):
            act.wait_ge(w_in, 16 * 18)
            act.activation(tgate[:, :], gates[:, :], ACT.Tanh).then_inc(tgate_ready, 1)

            def prep(s, B):
                for c0, n in ((0, 2 * BANK), (2 * BANK, CTX - 2 * BANK)):
                    k = B.next()
                    act.wait_ge(b_full, B.done())
                    act.activation(k1T[s][:, c0:c0 + n], pB[k][:, 0:n], ACT.Identity, bias=bcol[:, 3:4])\
                        .then_inc(b_done, 1)

            def exps(B):
                for i in range(NG):
                    for t in range(KT):
                        n = i * KT + t
                        k, kr = B.next(), tile_rows(t)
                        act.wait_ge(b_full, B.done())
                        act.activation(probs[n % 2][0:kr, :], pB[k][0:kr, :], ACT.Exp, scale=HD ** -0.5)\
                            .then_inc(b_done, 1)

            def hidden(B, r, func, bias):
                k = B.next()
                act.wait_ge(b_full, B.done())
                for c in range(HC):
                    last = act.activation(hid[r][:, c, :], pB[k][:, c * SEQ:(c + 1) * SEQ], func, bias=bias(c))
                last.then_inc(b_done, 1)

            def moe0(B, n):
                hidden(B, 0, ACT.Silu, lambda c: rb1[:, c:c + 1])
                for e in range(EXPERTS):
                    hidden(B, (e + 1) % 2, ACT.Silu, lambda c: b1[0][:, e, c:c + 1])
                    if e == 1:
                        act.wait_ge(dm_ready, n)
                        act.activation(tm[:, :], dm[:, :], ACT.Tanh, scale=0.5).then_inc(tm_ready, 1)

            def attn1(n):
                for r in range(QT):
                    act.wait_ge(nm1_ready, n + r + 1)
                    act.activation(sc1[r][:, :], sc1[r][:, :], ACT.Exp, bias=nm1[:, r:r + 1],
                                   accum_out=sum1[:, r:r + 1]).then_inc(p1_ready, 1)

            def moe1(B, n):
                act.wait_ge(nmg_ready, n)
                for r in range(QT):
                    last = act.activation(eg[:, r, :], lg[:, r, :], ACT.Exp, bias=nmg[:, r:r + 1],
                                          accum_out=sumg[:, r:r + 1])
                last.then_inc(eg_ready, 1)
                for e in range(EXPERTS):
                    hidden(B, (e + 1) % 2, ACT.Gelu, lambda c: b1[1][:, e, c:c + 1])

            B = Ring(0, 2)
            prep(0, B)
            prep(1, B)
            act.wait_ge(we_in, 16 * 8)

            def body(j, last):
                B = Ring(2 * B_PREP + B_BODY * j, 2)
                exps(B)
                moe0(B, 2 * j + 1)
                moe0(B, 2 * j + 2)
                attn1(4 * j)
                attn1(4 * j + 2)
                for s in range(2):
                    moe1(B, 2 * j + s + 1)
                    if not last:
                        prep(s, B)
                assert last or B.n == B_BODY

            with act.Fori(0, PAIRS - 1) as j:
                body(j, False)
            body(PAIRS - 1, True)

        @block.tensor
        def _(pe):
            mm = nc.tensor.matmul

            def open_a(A):
                k = A.next()
                pe.wait_ge(a_done, A.reusable())
                return pA[k]

            def open_b(B):
                k = B.next()
                pe.wait_ge(b_done, B.reusable())
                return pB[k]

            def transpose_y(s, A, n):
                bank = open_a(A)
                pe.wait_ge(y_ready, n)
                for r in range(QT):
                    last = nc.tensor.transpose(bank[:, r * PART:(r + 1) * PART], y[s][:, r, :], ident[:, :])
                last.then_inc(a_full, 1)

            def prep(s, A, B, n, yn):
                pe.wait_ge(ctx_in, 16 * n)
                for c0, w in CHUNKS:
                    bank = open_a(A)
                    mm(bank[:, 0:w], wk0[:, :], ctxT[:, c0:c0 + w], start=True, stop=True).then_inc(a_full, 1)
                for c0, w in ((0, 2 * BANK), (2 * BANK, CTX - 2 * BANK)):
                    banks = open_b(B)
                    for o in range(0, w, BANK):
                        m = min(BANK, w - o)
                        last = mm(banks[:, o:o + m], wk1[:, :], ctxT[:, c0 + o:c0 + o + m], start=True, stop=True)
                    last.then_inc(b_full, 1)
                for t0 in range(0, KT, 2):
                    bank = open_a(A)
                    for t in range(t0, min(t0 + 2, KT)):
                        kr = tile_rows(t)
                        last = mm(bank[0:kr, (t - t0) * 2 * DIM:(t - t0 + 1) * 2 * DIM],
                                  ctxT[:, t * PART:t * PART + kr], wv[:, :], start=True, stop=True)
                    last.then_inc(a_full, 1)
                transpose_y(s, A, yn)
                bank = open_a(A)
                pe.wait_ge(a_done, A.done() - 1)
                mm(bank[:, 0:SEQ], wq0[:, :], yT[s][:, :], start=True, stop=True).then_inc(a_full, 1)

            def scores_for_max(i, u, A):
                h, r, st = u // QT, u % QT, i % STAGES
                for c0, w in CHUNKS:
                    bank = open_a(A)
                    mm(bank[:, 0:w], qst[st][:, h, 0, r * PART:(r + 1) * PART], kst[st][:, c0:c0 + w],
                       start=True, stop=True).then_inc(a_full, 1)

            def wait_stage(i, j):
                pe.wait_ge(stage_in[i % STAGES], 16 * (1 + 2 * GH) * (2 * j + i // STAGES + 1))

            def attn0(A, B, j):
                mw_done = {}

                def event(kind, i, u):
                    if kind == "s1":
                        if u == 0:
                            wait_stage(i, j)
                        scores_for_max(i, u, A)
                    elif kind == "mw":
                        bank = open_a(A)
                        pe.wait_ge(mw_ready, NG * j + i + 1)
                        for r in range(QT):
                            last = nc.tensor.transpose(bank[:, r * PART:(r + 1) * PART], mw[:, r, :], ident[:, :])
                        last.then_inc(a_full, 1)
                        mw_done[i] = A.done()
                    elif kind == "ot":
                        bank = open_a(A)
                        pe.wait_ge(pv_done, NG * j + i + 2)
                        for r in range(QT):
                            last = nc.tensor.transpose(bank[:, r * PART:(r + 1) * PART],
                                                       oTs[:, r * PART:(r + 1) * PART], ident[:, :])
                        last.then_inc(a_full, 1)
                        mw_done["ot"] = A.done()
                    elif kind == "at":
                        bank = open_a(A)
                        pe.wait_ge(a_done, mw_done["ot"])
                        for r in range(QT):
                            last = nc.tensor.transpose(bank[:, r * PART:(r + 1) * PART], attn[:, r, :], ident[:, :])
                        last.then_inc(a_full, 1)
                        mw_done["at"] = A.done()
                    elif kind == "op":
                        bank = open_a(A)
                        pe.wait_ge(a_done, mw_done["at"])
                        for r in range(QT):
                            last = mm(bank[:, r * DIM:(r + 1) * DIM], attnT[:, r * PART:(r + 1) * PART], wo0[:, :],
                                      start=True, stop=True)
                        last.then_inc(a_full, 1)

                def weigh(n):
                    i, t = n // KT, n % KT
                    kr, s = tile_rows(t), i // GROUPS
                    if t == 0:
                        pe.wait_ge(pv_done, NG * j + i + 1)
                    pe.wait_ge(b_done, B.base + n + 1)
                    for h in range(GH):
                        last = mm(pO[ROWS * h:ROWS * h + HD + 1, 0:SEQ],
                                  vst[s][0:kr, t, (i % GROUPS) * GH + h, :],
                                  probs[n % 2][0:kr, h * SEQ:(h + 1) * SEQ], start=(t == 0), stop=(t == KT - 1))
                    if t == KT - 1:
                        last.then_inc(pv_full, 1)

                for u in range(2 * GH):
                    event("s1", 0, u)
                event("mw", 0, 0)
                for i in range(NG):
                    for t in range(KT):
                        n, kr = i * KT + t, tile_rows(t)
                        banks = open_b(B)
                        if t == 0:
                            pe.wait_ge(a_done, mw_done[i])
                        for hh in range(0, GH, 2):
                            last = mm(banks[0:kr, hh * SEQ:(hh + 2) * SEQ], kst[i % STAGES][:, t * PART:t * PART + kr],
                                      qst[i % STAGES][:, hh:hh + 2, 1, :], start=True, stop=True)
                        last.then_inc(b_full, 1)
                        for e in attention_events(i, t):
                            event(*e)
                        if n:
                            weigh(n - 1)
                weigh(NG * KT - 1)
                event("ot", NG - 1, 0)
                event("at", 1, 0)
                event("op", 1, 0)

            def moe(l, s, A, B, n):
                first = B.n

                def up(e):
                    banks = open_b(B)
                    for c in range(HC):
                        lhs = rw1[:, c * PART:(c + 1) * PART] if e < 0 else w1[l][:, e, c * PART:(c + 1) * PART]
                        last = mm(banks[:, c * SEQ:(c + 1) * SEQ], lhs, yT[s][:, :], start=True, stop=True)
                    last.then_inc(b_full, 1)

                def down(e):
                    bank = open_a(A)
                    k = e + 1 + (l == 0)
                    pe.wait_ge(b_done, B.base + first + k)
                    for r in range(QT):
                        for c in range(HC):
                            last = mm(bank[:, r * DIM:(r + 1) * DIM], hid[(e + 1) % 2][:, c, r * PART:(r + 1) * PART],
                                      w2[l][:, e, c, :], start=(c == 0), stop=(c == HC - 1))
                    last.then_inc(a_full, 1)

                pe.wait_ge(a_done, A.done())
                if l == 0:
                    up(-1)
                    up(0)
                    bank = open_a(A)
                    pe.wait_ge(b_done, B.base + first + 1)
                    for r in range(QT):
                        for c in range(HC):
                            last = mm(bank[:, r * EXPERTS:(r + 1) * EXPERTS], hid[0][:, c, r * PART:(r + 1) * PART],
                                      rw2[:, c, :], start=(c == 0), stop=(c == HC - 1))
                    last.then_inc(a_full, 1)
                else:
                    bank = open_a(A)
                    for r in range(QT):
                        last = mm(bank[:, r * EXPERTS:(r + 1) * EXPERTS], yT[s][:, r * PART:(r + 1) * PART], wg[:, :],
                                  start=True, stop=True)
                    last.then_inc(a_full, 1)
                    up(0)
                for e in range(1, EXPERTS):
                    up(e)
                    down(e - 1)
                down(EXPERTS - 1)
                bank = open_a(A)
                pe.wait_ge(we_ready, n)
                for r in range(QT):
                    last = nc.tensor.transpose(bank[0:EXPERTS, r * PART:(r + 1) * PART], we[:, r, :], ident[:, :])
                last.then_inc(a_full, 1)
                bank = open_a(A)
                pe.wait_ge(a_done, A.done() - 1)
                for r in range(QT):
                    last = mm(bank[:, r * DIM:(r + 1) * DIM], weT[:, r, :], b2[l][:, :], start=True, stop=True)
                last.then_inc(a_full, 1)

            def attn1(s, A, n):
                bank = open_a(A)
                pe.wait_ge(a_done, A.done() - 1)
                mm(bank[:, 0:SEQ], wq1[:, :], yT[s][:, :], start=True, stop=True).then_inc(a_full, 1)
                q_at = A.done()
                for r in range(QT):
                    for c0, w in CHUNKS:
                        bank = open_a(A)
                        pe.wait_ge(a_done, q_at)
                        mm(bank[:, 0:w], q1T[:, r * PART:(r + 1) * PART], k1T[s][:, c0:c0 + w],
                           start=True, stop=True).then_inc(a_full, 1)
                for r in range(QT):
                    pe.wait_ge(p1_ready, n + r + 1)
                    for t0 in range(0, KT, 4):
                        bank = open_a(A)
                        for t in range(t0, min(t0 + 4, KT)):
                            kr = tile_rows(t)
                            last = nc.tensor.transpose(bank[0:kr, (t - t0) * PART:(t - t0 + 1) * PART],
                                                       sc1[r][:, t * PART:t * PART + kr], ident[:, :])
                        last.then_inc(a_full, 1)
                    bank = open_a(A)
                    pe.wait_ge(a_done, A.done() - 1)
                    for t in range(KT):
                        kr = tile_rows(t)
                        last = mm(bank[:, 0:DIM], p1T[0:kr, t, :], v1[s][0:kr, t, :], start=(t == 0), stop=(t == KT - 1))
                    last.then_inc(a_full, 1)

            pe.wait_ge(w_in, 16 * 18)
            pe.wait_ge(zeroed, 2)
            A, B = Ring(0, 3), Ring(0, 2)
            prep(0, A, B, 1, 1)
            prep(1, A, B, 2, 2)
            pe.wait_ge(we_in, 16 * 8)

            def body(j, last):
                A, B = Ring(2 * A_PREP + A_BODY * j, 3), Ring(2 * B_PREP + B_BODY * j, 2)
                yn = 2 + 8 * j
                attn0(A, B, j)
                for s in range(2):
                    transpose_y(s, A, yn + s + 1)
                    moe(0, s, A, B, 4 * j + s + 1)
                for s in range(2):
                    transpose_y(s, A, yn + 2 + s + 1)
                    attn1(s, A, 4 * j + 2 * s)
                for s in range(2):
                    transpose_y(s, A, yn + 4 + s + 1)
                    moe(1, s, A, B, 4 * j + 2 + s + 1)
                    if not last:
                        prep(s, A, B, 2 * (j + 1) + s + 1, yn + 6 + s + 1)
                assert last or (A.n == A_BODY and B.n == B_BODY), (A.n, A_BODY, B.n, B_BODY)

            with pe.Fori(0, PAIRS - 1) as j:
                body(j, False)
            body(PAIRS - 1, True)


        @block.vector
        def _(dve):
            v = nc.vector
            links = [0, 0]

            def link(ins, alone=False):
                links[1] += 1
                ins.then_inc(chain, 1)
                dve.wait_ge(chain, links[0] + links[1])
                if alone:
                    dve.sem_inc(passed, 1)

            def next_a(A, alone=False):
                k = A.next()
                dve.wait_ge(a_full, A.done())
                if alone:
                    dve.sem_inc(passed, 1)
                return pA[k]

            def layer_norm(s, n):
                for r in range(QT):
                    last = v.bn_stats(bst[:, r, :], xres[s][:, r, :])
                link(last, alone=True)
                for r in range(QT):
                    last = v.bn_aggr(mv[:, r, :], bst[:, r, :])
                link(last)
                v.tensor_scalar(vpe[:, :], mv[:, :, 1], EPS, None, ALU.add).then_inc(var_ready, 1)
                dve.wait_ge(rstd_ready, n)
                link(v.tensor_tensor(nt1[:, :], rst[:, :], rst[:, :], ALU.mult))
                link(v.tensor_tensor(nt2[:, :], nt1[:, :], vpe[:, :], ALU.mult))
                link(v.tensor_scalar(nt1[:, :], nt2[:, :], -0.5, 1.5, ALU.mult, ALU.add))
                link(v.tensor_tensor(rr[:, :], nt1[:, :], rst[:, :], ALU.mult))
                for r in range(QT):
                    last = v.tensor_scalar(y[s][:, r, :], xres[s][:, r, :], mv[:, r, 0:1], rr[:, r:r + 1],
                                           ALU.subtract, ALU.mult)
                last.then_inc(y_ready, 1)

            def keep(dst, A):
                bank = next_a(A)
                v.tensor_copy(dst[:, :], bank[:, 0:SEQ]).then_inc(a_done, 1)

            def prep(s, A, xn, stored, yn):
                dve.wait_ge(k_stored, 48 * stored)
                for c0, w in CHUNKS:
                    bank = next_a(A)
                    link(v.tensor_scalar(khi[:, c0:c0 + w], bank[:, 0:w], bcol[:, 1:2], None, ALU.add))
                    v.scalar_tensor_tensor(klo[:, c0:c0 + w], bank[:, 0:w], bcol[:, 1:2], khi[:, c0:c0 + w],
                                           op0=ALU.add, op1=ALU.subtract).then_inc(a_done, 1)
                dve.wait_ge(x_in[s], 16 * xn)
                layer_norm(s, yn)
                for t0 in range(0, KT, 2):
                    bank = next_a(A)
                    for t in range(t0, min(t0 + 2, KT)):
                        kr = tile_rows(t)
                        src = bank[0:kr, (t - t0) * 2 * DIM:(t - t0 + 1) * 2 * DIM]
                        v.tensor_tensor(vst[s][0:kr, t, :, 0:HD], src[:, 0:DIM].rearrange("p (h c) -> p h c", c=HD),
                                        bv[0:kr, 0:DIM].rearrange("p (h c) -> p h c", c=HD), ALU.add)
                        last = v.tensor_tensor(v1[s][0:kr, t, :], src[:, DIM:2 * DIM], bv[0:kr, DIM:2 * DIM], ALU.add)
                    last.then_inc(a_done, 1)
                keep(yT[s], A)
                bank = next_a(A)
                dve.wait_ge(q_stored, 48 * stored)
                link(v.tensor_scalar(qhi[:, :], bank[:, 0:SEQ], bcol[:, 0:1], None, ALU.add))
                v.scalar_tensor_tensor(qlo[:, :], bank[:, 0:SEQ], bcol[:, 0:1], qhi[:, :],
                                       op0=ALU.add, op1=ALU.subtract).then_inc(a_done, 1)

            def attn0(A, j, yn):
                mw_of = mw[:, :, :].rearrange("p q (h r) -> p h q r", h=GH)

                def event(kind, i, u):
                    if kind == "s1":
                        for c, (c0, w) in enumerate(CHUNKS):
                            bank = next_a(A)
                            v.reduce_max(mxp[:, u, c:c + 1], bank[:, 0:w], axis=AX.X).then_inc(a_done, 1)
                    elif kind == "mw":
                        dve.wait_ge(a_done, A.done())
                        link(v.tensor_reduce(mw_of[:, :, :, 0], mxp[:, :, :].rearrange("p (h q) c -> p h q c", h=GH),
                                             axis=AX.X, op=ALU.max, negate=True))
                        link(v.tensor_scalar(m16[:, :, :], mw_of[:, :, :, 0], 1 / MAX_SCALE, None, ALU.mult))
                        v.scalar_tensor_tensor(mw_of[:, :, :, 1], m16[:, :, :], -MAX_SCALE, mw_of[:, :, :, 0],
                                               op0=ALU.mult, op1=ALU.add).then_inc(mw_ready, 1)
                        bank = next_a(A)
                        for h in range(GH):
                            p = ROWS * h
                            last = v.tensor_scalar(qst[i % STAGES][p:p + 2, h, 1, :], bank[p:p + 2, 0:SEQ],
                                                   1 / MAX_SCALE, None, ALU.mult)
                        last.then_inc(a_done, 1)
                    elif kind == "ot":
                        bank = next_a(A)
                        o = bank[:, 0:SEQ].rearrange("p (q h r) -> p q h r", q=QT, h=GH)
                        link(v.reciprocal(rec[:, :, :], o[:, :, :, HD]))
                        g = i % GROUPS
                        dst = attn[:, :, g * GH * HD:(g + 1) * GH * HD].rearrange("p q (h c) -> p q h c", c=HD)
                        v.tensor_tensor(dst, o[:, :, :, 0:HD], rec[:, :, :].unsqueeze(3).broadcast_to([PART, QT, GH, HD]),
                                        ALU.mult).then_inc(a_done, 1)
                    elif kind == "at":
                        keep(attnT, A)
                    elif kind == "op":
                        bank = next_a(A)
                        for r in range(QT):
                            last = v.tensor_tensor(oproj[:, r, :], bank[:, r * DIM:(r + 1) * DIM], bo[:, :], ALU.add)
                        last.then_inc(a_done, 1)
                        dve.wait_ge(a_done, A.done())
                        link(v.scalar_tensor_tensor(xres[i][:, :, :], oproj[:, :, :], tgate[:, 0:1], xres[i][:, :, :],
                                                    op0=ALU.mult, op1=ALU.add))
                        layer_norm(i, yn + i + 1)

                def copy_outputs(i):
                    dve.wait_ge(pv_full, NG * j + i + 1)
                    v.tensor_copy(oTs[:, :], pO[:, 0:SEQ]).then_inc(pv_done, 1)

                for u in range(2 * GH):
                    event("s1", 0, u)
                event("mw", 0, 0)
                for i in range(NG):
                    for t in range(KT):
                        if t == 1 and i > 0:
                            copy_outputs(i - 1)
                        for e in attention_events(i, t):
                            event(*e)
                copy_outputs(NG - 1)
                event("ot", NG - 1, 0)
                event("at", 1, 0)
                event("op", 1, 0)

            def top_two(l, n):
                for r in range(QT):
                    last = v.max(m8[:, r, :], lg[:, r, :])
                link(last)
                if l == 0:
                    v.tensor_tensor(dm[:, :], m8[:, :, 0], m8[:, :, 1], ALU.subtract).then_inc(dm_ready, 1)
                else:
                    v.tensor_scalar(nmg[:, :], m8[:, :, 0], -1.0, None, ALU.mult).then_inc(nmg_ready, 1)
                for r in range(QT):
                    last = v.max_index(i8[:, r, :], m8[:, r, :], lg[:, r, :])
                link(last)
                link(v.tensor_copy(i8f[:, :, :], i8[:, :, 0:2]))
                if l == 0:
                    dve.wait_ge(tm_ready, n)
                    v.tensor_scalar(pr[:, :, 0], tm[:, :], 0.5, 0.5, ALU.mult, ALU.add)
                    link(v.tensor_scalar(pr[:, :, 1], tm[:, :], -0.5, 0.5, ALU.mult, ALU.add))
                else:
                    dve.wait_ge(eg_ready, n)
                    link(v.reciprocal(rg[:, :], sumg[:, :]))
                for r in range(QT):
                    for k in range(2):
                        w = pr[:, r, k:k + 1] if l == 0 else rg[:, r:r + 1]
                        last = v.tensor_scalar(oh[:, r, k, :], iota[:, :], i8f[:, r, k:k + 1], w,
                                               ALU.is_equal, ALU.mult)
                link(last)
                if l == 0:
                    v.tensor_tensor(we[:, :, :], oh[:, :, 0, :], oh[:, :, 1, :], ALU.add).then_inc(we_ready, 1)
                else:
                    link(v.tensor_tensor(oh[:, :, 0, :], oh[:, :, 0, :], oh[:, :, 1, :], ALU.add))
                    v.tensor_tensor(we[:, :, :], oh[:, :, 0, :], eg[:, :, :], ALU.mult).then_inc(we_ready, 1)

            def moe(l, s, A, j, n, wn):
                bank = next_a(A)
                for r in range(QT):
                    src = bank[:, r * EXPERTS:(r + 1) * EXPERTS]
                    last = (v.tensor_tensor(lg[:, r, :], src, rb2[:, :], ALU.add) if l == 0
                            else v.tensor_copy(lg[:, r, :], src))
                last.then_inc(a_done, 1)
                dve.wait_ge(a_done, A.done())
                dve.sem_inc(passed, 1)
                top_two(l, n)
                dve.wait_ge(we_ready, wn)
                for e in range(EXPERTS):
                    bank = next_a(A)
                    dve.wait_ge(a_done, A.done() - 1)
                    for r in range(QT):
                        src = bank[:, r * DIM:(r + 1) * DIM]
                        if e == 0:
                            last = v.tensor_scalar(acc[:, r, :], src, we[:, r, e:e + 1], None, ALU.mult)
                        else:
                            last = v.scalar_tensor_tensor(acc[:, r, :], src, we[:, r, e:e + 1], acc[:, r, :],
                                                          op0=ALU.mult, op1=ALU.add)
                    last.then_inc(a_done, 1)
                bank = next_a(A)
                v.tensor_copy(weT[:, :, :], bank[0:EXPERTS, 0:SEQ].rearrange("e (q p) -> e q p", q=QT)).then_inc(a_done, 1)
                bank = next_a(A)
                dve.wait_ge(a_done, A.done() - 1)
                v.tensor_tensor(acc[:, :, :], bank[:, 0:QT * DIM].rearrange("p (q d) -> p q d", q=QT), acc[:, :, :],
                                ALU.add).then_inc(a_done, 1)
                dve.wait_ge(a_done, A.done())
                if l == 1:
                    dve.wait_ge(out_stored[s], 16 * (j + 1))
                ins = v.scalar_tensor_tensor((xres if l == 0 else xout)[s][:, :, :], acc[:, :, :],
                                             tgate[:, 2 + l:3 + l], xres[s][:, :, :], op0=ALU.mult, op1=ALU.add)
                if l == 0:
                    link(ins)
                else:
                    ins.then_inc(x_final, 1)

            def attn1(s, A, n):
                bank = next_a(A)
                v.tensor_scalar(q1T[:, :], bank[:, 0:SEQ], bcol[:, 2:3], DIM ** -0.5, ALU.add, ALU.mult)\
                    .then_inc(a_done, 1)
                for r in range(QT):
                    dve.wait_ge(side_scaled, n + r + 1)
                    for c, (c0, w) in enumerate(CHUNKS):
                        bank = next_a(A, alone=True)
                        v.tensor_tensor_reduce(out=sc1[r][:, c0:c0 + w], in0=bank[:, 0:w], in1=sc1[r][:, c0:c0 + w],
                                               scale=1.0, scalar=-3.0e38, op0=ALU.add, op1=ALU.max,
                                               accum_out=mx1[:, r, c:c + 1]).then_inc(a_done, 1)
                    dve.wait_ge(a_done, A.done())
                    v.tensor_reduce(nm1[:, r:r + 1], mx1[:, r, :], axis=AX.X, op=ALU.max, negate=True)\
                        .then_inc(nm1_ready, 1)
                for r in range(QT):
                    for t0 in range(0, KT, 4):
                        m = min(4, KT - t0)
                        kr = tile_rows(t0 + m - 1)
                        bank = next_a(A)
                        v.tensor_copy(p1T[0:kr, t0:t0 + m, :],
                                      bank[0:kr, 0:m * PART].rearrange("p (t q) -> p t q", t=m)).then_inc(a_done, 1)
                    dve.wait_ge(p1_ready, n + r + 1)
                    link(v.reciprocal(rs1[:, r:r + 1], sum1[:, r:r + 1]))
                    link(v.tensor_tensor(rs1[:, r:r + 1], rs1[:, r:r + 1], tgate[:, 1:2], ALU.mult))
                    bank = next_a(A)
                    v.scalar_tensor_tensor(xres[s][:, r, :], bank[:, 0:DIM], rs1[:, r:r + 1], xres[s][:, r, :],
                                           op0=ALU.mult, op1=ALU.add).then_inc(a_done, 1)
                dve.wait_ge(a_done, A.done())

            v.memset(mw[:, :, :], 0.0)
            for r in range(STAGES):
                v.memset(qst[r][:, :, :, :].bitcast(fp32), 0.0)
            for s in range(2):
                v.memset(vst[s][:, :, :, :], 1.0)
            v.memset(pO[:, :], 0.0).then_inc(pv_done, 1)
            dve.wait_ge(pv_done, 1)
            v.memset(rec[:, :, :], 0.0).then_inc(zeroed, 1)
            dve.wait_ge(w_in, 16 * 18)
            dve.wait_ge(zeroed, 2)
            link(v.tensor_tensor(betas[:, 3:4], betas[:, 0:1], betas[:, 1:2], ALU.add))
            v.tensor_tensor(betas[:, 3:4], betas[:, 3:4], betas[:, 2:3], ALU.subtract).then_inc(coef_ready, 1)
            dve.wait_ge(tgate_ready, 1)
            A = Ring(0, 3)
            prep(0, A, 1, 0, 1)
            prep(1, A, 1, 1, 2)
            pro, links[1] = links[1], 0

            def body(j, last):
                A = Ring(2 * A_PREP + A_BODY * j, 3)
                links[0], links[1] = pro + C_BODY * j, 0
                yn = 2 + 8 * j
                attn0(A, j, yn)
                keep(yT[0], A)
                moe(0, 0, A, j, 2 * j + 1, 4 * j + 1)
                keep(yT[1], A)
                layer_norm(0, yn + 3)
                moe(0, 1, A, j, 2 * j + 2, 4 * j + 2)
                keep(yT[0], A)
                layer_norm(1, yn + 4)
                attn1(0, A, 4 * j)
                keep(yT[1], A)
                layer_norm(0, yn + 5)
                attn1(1, A, 4 * j + 2)
                keep(yT[0], A)
                layer_norm(1, yn + 6)
                moe(1, 0, A, j, 2 * j + 1, 4 * j + 3)
                if not last:
                    prep(0, A, j + 2, 2 * j + 2, yn + 7)
                keep(yT[1], A)
                moe(1, 1, A, j, 2 * j + 2, 4 * j + 4)
                if not last:
                    prep(1, A, j + 2, 2 * j + 3, yn + 8)
                assert last or (A.n == A_BODY and links[1] == C_BODY), (A.n, A_BODY, links[1], C_BODY)

            with dve.Fori(0, PAIRS - 1) as j:
                body(j, False)
            body(PAIRS - 1, True)


def kernel(**inputs):
    import numpy as np
    import concourse.bacc as bacc
    from concourse import mybir as mb
    from concourse.bass_utils import run_bass_kernel_spmd as run

    a = {k: np.asarray(v) for k, v in inputs.items()}

    def col(*names):
        return np.stack([a[n].reshape(DIM) for n in names], 1)

    def row(v):
        return np.broadcast_to(v.reshape(1, -1), (PART, v.size))

    def chunked(v):
        return np.moveaxis(v.reshape(v.shape[:-1] + (HC, PART)), -1, 0)

    kpad = np.zeros((HEADS, HD, CTX), np.float16)
    kpad[:, 0:2] = MAX_SCALE
    io = {
        "x": a["x"], "side": a["fside_BxSxS2_0"], "ctxT": a["ctx_1024"].transpose(0, 2, 1),
        "ident": np.eye(PART, dtype=np.float32), "iota": row(np.arange(EXPERTS, dtype=np.float32)),
        "kpad": kpad, "qpad": np.zeros((HEADS, HD, SEQ), np.float16),
        "wk0": a["L0_xattn_Wk"], "wq0": a["L0_xattn_Wq"], "wo0": a["L0_xattn_Wo"],
        "wk1": a["L1_xattn_Wk"].T, "wq1": a["L1_xattn_Wq"].T,
        "wv": np.concatenate([a["L0_xattn_Wv"], a["L1_xattn_Wv"].T], 1),
        "bcol": col("L0_xattn_bq", "L0_xattn_bk", "L1_xattn_bq", "L1_xattn_bk"),
        "bv": row(np.concatenate([a["L0_xattn_bv"], a["L1_xattn_bv"]])), "bo": row(a["L0_xattn_bo"]),
        "gates": row(np.concatenate([a["g_xattn"], a["g_ffn"]])),
        "betas": row(np.stack([a[f"L1_xattn_beta_{n}"].reshape(()) for n in ("risk", "prio", "impl")])),
        "rb1": chunked(a["L0_ffn_rb1"]), "rb2": row(a["L0_ffn_rb2"]), "rw1": a["L0_ffn_rw1"],
        "wg": a["L1_ffn_w_gate"].T, "rw2": a["L0_ffn_rw2"].reshape(HC, PART, EXPERTS).transpose(1, 0, 2),
    }
    for l, (n1, nb1, n2, nb2) in enumerate((("w1", "b1", "w2", "b2"), ("W1", "b1", "W2", "b2"))):
        io[f"w1_{l}"] = a[f"L{l}_ffn_{n1}"].transpose(1, 0, 2)
        io[f"b1_{l}"] = chunked(a[f"L{l}_ffn_{nb1}"])
        io[f"w2_{l}"] = a[f"L{l}_ffn_{n2}"].reshape(EXPERTS, HC, PART, DIM).transpose(2, 0, 1, 3)
        io[f"b2_{l}"] = a[f"L{l}_ffn_{nb2}"]

    nc = bacc.Bacc("TRN2", target_bir_lowering=False, num_devices=1)
    arrays, aps = {}, {}
    for name, v in io.items():
        v = np.ascontiguousarray(v)
        arrays[f"in_{name}"] = v
        aps[name] = nc.dram_tensor(f"in_{name}", v.shape, mb.dt.from_np(v.dtype), kind="ExternalInput").ap()
    out = nc.dram_tensor("out_0", (BATCH, SEQ, DIM), mb.dt.float32, kind="ExternalOutput").ap()
    flamingo(nc, aps, out)
    r = run(nc, [arrays], core_ids=[0])
    return r.results[0]["out_0"]
```

```python
import concourse.bass as bass
from concourse import mybir
from contextlib import ExitStack

BATCH, SEQ, CTX, DIM = 8, 256, 1601, 128
HEADS, HD = 16, 8
EXPERTS, HID = 8, 512
PART = 128
QT = SEQ // PART
KT = -(-CTX // PART)
HC = HID // PART
PAIRS = BATCH // 2
BANK = 512
CHUNKS = [(c, min(BANK, CTX - c)) for c in range(0, CTX, BANK)]
GH = 4
GROUPS = HEADS // GH
NG = 2 * GROUPS
ROWS = PART // GH
W_SCALE, Y_SCALE = 2.0 ** 8, 2.0 ** 11
UNSCALE = 1 / (W_SCALE * Y_SCALE)
HALVES = ((0, 0), (0, 1), (1, 0))
MAX_SCALE = 64.0
STAGES = 4
EPS = 1e-5


def tile_rows(t):
    return min(PART, CTX - t * PART)


PUT_AFTER = 6
WEIGHTS_FIRST = 3
PRE = 2


def prepare(s):
    keys = [("keys0", s, c) for c in range(len(CHUNKS))]
    return (keys[:2] + [("norm", s, "q")] + keys[2:] + [("finish", s, "q"), ("keys1", s, 0), ("turn", s, "q"), ("keys1", s, 1),
            ("query0", s)] + [("values", s, t) for t in range(0, KT, 4)])


def maxima(groups):
    steps = []
    for i in groups:
        chunks = [("s1", i, u, c) for u in range(2 * GH) for c in range(len(CHUNKS))]
        steps += chunks[:PUT_AFTER] + ([("put_max", i - 1)] if i > groups[0] else []) + chunks[PUT_AFTER:]
        steps.append(("split_max", i))
    return steps, [("put_max", groups[-1])]


def hidden(l, s):
    return [(l, s, e) for e in range(-1 if l == 0 else 0, EXPERTS)]


def weave(steps, fills):
    at = {}
    for first, last, more in fills:
        a, b = int(first * len(steps)), int(last * len(steps))
        for k, step in enumerate(more):
            at.setdefault(a + k * (b - a) // len(more), []).append(step)
    return [x for n, step in enumerate(steps) for x in [step] + at.get(n, [])]


def prologue():
    chunks, put = maxima(range(PRE))
    return prepare(0) + [("split", n) for n in range(WEIGHTS_FIRST)] + chunks + put


def attention0():
    steps = []
    for n in range(KT * NG):
        i, t = n // KT, n % KT
        steps.append(("s2", i, t))
        if t == 3 and i:
            steps.append(("turn_out", i - 1))
        if i == NG - 3 and t < 4:
            steps.append(("scale_side", t))
        if i == GROUPS:
            steps += {5: [("turn_attn", 0)], 6: [("project", 0)], 7: [("norm", 0, "m0")], 9: [("finish", 0, "m0")],
                      11: [("turn", 0, "m0")]}.get(t, [])
        if n:
            steps.append(("weigh", (n - 1) // KT, (n - 1) % KT))
        if t == 0 and i:
            steps.append(("keep_out", i - 1))
    chunks, put = maxima(range(PRE, NG))
    return weave(steps, [(0.0, 0.17, prepare(1)), (0.0, 0.845, chunks + put)])


def experts(ups, beside, before_down=()):
    steps = []
    for k, (l, s, e) in enumerate(ups):
        steps += [("up", l, s, e, c) for c in range(HC)]
        if k in before_down:
            steps += beside[k]
        if k and ups[k - 1][2] == 0:
            steps.append(("pick", *ups[k - 1][:2]))
        if k:
            steps.append(("down",) + ups[k - 1])
            if ups[k - 1][2] < 0:
                steps.append(("tanh", ups[k - 1][1]))
        if k not in before_down:
            steps += beside.get(k, [])
    return steps


def pair(last):
    steps = attention0()

    ups = hidden(0, 0) + hidden(0, 1)
    steps += experts(ups, {
        0: [("weigh", NG - 1, KT - 1), ("keep_out", NG - 1)], 1: [("turn_out", NG - 1)], 2: [("turn_attn", 1)],
        3: [("project", 1), ("norm", 1, "m0")], 4: [("finish", 1, "m0")], 6: [("turn", 1, "m0")],
        9: [("turn_we", 0, 0)], 10: [("bias2", 0, 0), ("norm", 0, "a1")], 11: [("finish", 0, "a1")],
        12: [("turn", 0, "a1")], 13: [("query1", 0)],
        14: [("qk", 0, c) for c in (0, 1)], 15: [("qk", 0, c) for c in (2, 3)] + [("max1", 0)],
        16: [("qk", 1, c) for c in (0, 1)], 17: [("qk", 1, c) for c in (2, 3)] + [("max1", 1)],
    }, before_down=(9,))
    turns = lambda k: [("turn_p", k, b) for b in range(-(-KT // 4))]
    qk = lambda k: [("qk", k, c) for c in range(len(CHUNKS))] + [("max1", k)]
    steps += [("exp1", 0), ("exp1", 1), ("down",) + ups[-1], ("turn_we", 0, 1)] + turns(0)
    steps += [("bias2", 0, 1), ("norm", 1, "a1"), ("out1", 0)] + turns(1)[:2] + [("finish", 1, "a1")] + turns(1)[2:]
    steps += [("turn", 1, "a1"), ("out1", 1), ("query1", 1), ("norm", 0, "m1")] + qk(2)
    steps += [("exp1", 2), ("finish", 0, "m1")] + qk(3) + [("exp1", 3), ("turn", 0, "m1")] + turns(2)
    steps += [("gate", 0), ("out1", 2), ("exp_gate", 0)] + turns(3) + [("out1", 3), ("norm", 1, "m1")]

    ups = hidden(1, 0) + hidden(1, 1)
    moe = experts(ups, {0: [("finish", 1, "m1")], 2: [("turn", 1, "m1")], 3: [("gate", 1), ("exp_gate", 1)],
                        8: [("turn_we", 1, 0)], 9: [("bias2", 1, 0)]}, before_down=(8,))
    if not last:
        chunks, put = maxima(range(NG, NG + PRE))
        moe = weave(moe, [(0.08, 0.28, prepare(0)), (0.42, 0.96, chunks + put)])
    return steps + moe + [("down",) + ups[-1], ("turn_we", 1, 1), ("bias2", 1, 1)]


LAST_VALUES = (KT - 1) // 4 * 4
ON_A = {"keys0", "turn", "query0", "s1", "put_max", "turn_out", "turn_attn", "project", "down", "turn_we",
        "bias2", "query1", "qk", "turn_p", "out1", "gate"}
ON_B = {"keys1", "values", "s2", "up"}


class Plan:

    def __init__(self, steps):
        self.steps, self.count, self.at = steps, {}, {}
        for step in steps:
            if step[0] == "up" and step[-1] < HC - 1:
                continue
            for name in (["A"] if step[0] in ON_A else ["B"] if step[0] in ON_B else []) + [step[0]]:
                self.count[name] = self.count.get(name, 0) + 1
                self.at[name, step] = self.count[name]
        self.count["links"] = sum(LINKS.get(k, lambda *a: 0)(*a) for k, *a in steps)

    def unit(self, ring, step):
        return self.at[ring, ("up", *step[1:4], HC - 1) if step[0] == "up" else step]


LINKS = {"keys0": lambda *a: 1, "norm": lambda *a: 2, "finish": lambda *a: 4, "pick": lambda l, s: 3 if l else 2, "query0": lambda *a: 1, "query1": lambda *a: 1,
         "turn": lambda s, what: 1 if what in ("m0", "m1") else 0, "split_max": lambda *a: 2,
         "turn_out": lambda *a: 1, "project": lambda *a: 1, "down": lambda l, s, e: 3 if e < 0 else 0,
         "gate": lambda *a: 3, "bias2": lambda l, s: 1 if l == 0 else 0, "out1": lambda *a: 2}
PROLOGUE, PAIR, LAST = Plan(prologue()), Plan(pair(False)), Plan(pair(True))


def before(name, j, plan=PAIR):
    if plan is PROLOGUE:
        return 0
    return PROLOGUE.count.get(name, 0) + PAIR.count.get(name, 0) * j


SPLITS = [(e, f"w1_{l}") for l in range(2) for e in range(EXPERTS)]
SPLITS = [[(None, "rw1")]] + [SPLITS[n:n + 3] for n in range(0, 12, 3)] + [SPLITS[12:14], SPLITS[14:16], [(None, "wg")]]


def slot_number(plan, j, s):
    return 0 if plan is PROLOGUE else 2 * j + 2 - s


def free_at(base, n, depth):
    return base + max(n - depth, 0)


def flamingo(nc, io, out):
    fp32, fp16, u32 = mybir.dt.float32, mybir.dt.float16, mybir.dt.uint32
    ALU, ACT, AX = mybir.AluOpType, mybir.ActivationFunctionType, mybir.AxisListType
    ctx = ExitStack()
    with ctx:
        def sb(name, shape, dt=fp32):
            return ctx.enter_context(nc.sbuf_tensor(name, shape, dt))

        def sem(name):
            return ctx.enter_context(nc.semaphore(name))

        ident = sb("ident", [PART, PART])
        iota = sb("iota", [PART, EXPERTS])
        wk0, wq0, wo0, wk1, wq1 = (sb(n, [DIM, DIM]) for n in ("wk0", "wq0", "wo0", "wk1", "wq1"))
        wv = sb("wv", [DIM, 2 * DIM])
        rw2, wg = sb("rw2", [PART, HC, EXPERTS]), sb("wg", [DIM, EXPERTS])
        w1 = [[sb(f"w1_{l}{p}", [DIM, EXPERTS, HID], fp16) for p in ("hi", "lo")] for l in range(2)]
        rw1 = [sb(f"rw1{p}", [DIM, HID], fp16) for p in ("hi", "lo")]
        wg16 = [sb(f"wg{p}", [DIM, EXPERTS], fp16) for p in ("hi", "lo")]
        w2 = [sb(f"w2_{l}", [PART, EXPERTS, HC, DIM]) for l in range(2)]
        b1 = [sb(f"b1_{l}", [PART, EXPERTS, HC]) for l in range(2)]
        b2 = [sb(f"b2_{l}", [EXPERTS, DIM]) for l in range(2)]
        bcol = sb("bcol", [PART, 5])
        rb1 = sb("rb1", [PART, HC])
        bv1 = sb("bv1", [PART, DIM])
        bo = sb("bo", [PART, DIM])
        rb2 = sb("rb2", [PART, EXPERTS])
        gates = sb("gates", [PART, 4])
        tgate = sb("tgate", [PART, 4])
        betas = sb("betas", [PART, 4])
        neghalf = sb("neghalf", [PART, QT])

        xin = [sb(f"xin{s}", [PART, QT, DIM]) for s in range(2)]
        xres = [sb(f"xres{s}", [PART, QT, DIM]) for s in range(2)]
        yT = {0: sb("yT0", [DIM, SEQ]), 1: sb("yT1", [DIM, SEQ]), "q": sb("yTq", [DIM, SEQ])}
        y16 = [[yT[s][:, :].bitcast(fp16)[:, p * SEQ:(p + 1) * SEQ] for p in range(2)] for s in range(2)]
        y = {"q": sb("yq", [PART, QT, DIM]), "x": sb("yx", [PART, QT, DIM])}
        vst = [sb(f"vst{s}", [PART, KT, HEADS, HD + 1]) for s in range(2)]
        k1T = [sb(f"k1T{s}", [DIM, CTX]) for s in range(2)]
        v1 = [sb(f"v1_{s}", [PART, KT, DIM]) for s in range(2)]
        we = [sb(f"we{s}", [PART, QT, EXPERTS]) for s in range(2)]
        acc = [sb(f"acc{s}", [PART, QT, DIM]) for s in range(2)]
        oproj = acc[1]
        ctxT = sb("ctxT", [DIM, CTX])
        p1T = sb("p1T", [PART, KT, PART])
        halves = p1T[:, :, :].rearrange("p t q -> p (t q)").bitcast(fp16)
        khi, klo = halves[:, 0:CTX], halves[:, KT * PART:KT * PART + CTX]
        qhi, qlo = sb("qhi", [DIM, SEQ], fp16), sb("qlo", [DIM, SEQ], fp16)
        kst = [sb(f"kst{r}", [PART, CTX], fp16) for r in range(STAGES)]
        qst = [sb(f"qst{r}", [PART, GH, SEQ], fp16) for r in range(STAGES)]
        probs = [sb(f"probs{r}", [PART, GH * SEQ]) for r in range(2)]
        mxp = sb("mxp", [PART, 2 * GH, len(CHUNKS)])
        mw = sb("mw", [PART, QT, PART])
        m16 = sb("m16", [PART, GH, QT], fp16)
        oTs = sb("oTs", [PART, SEQ])
        rec = sb("rec", [PART, QT, GH])
        attn = sb("attn", [PART, QT, DIM])
        attnT = sb("attnT", [DIM, SEQ])
        hid = [sb(f"hid{r}", [PART, HC, SEQ]) for r in range(2)]
        q1T = sb("q1T", [DIM, SEQ])
        sc1 = [sb(f"sc1_{k}", [PART, CTX]) for k in range(2 * QT)]
        mx1 = sb("mx1", [PART, 2 * QT, len(CHUNKS)])
        nm1, sum1, rs1 = (sb(n, [PART, 2 * QT]) for n in ("nm1", "sum1", "rs1"))
        bst = sb("bst", [PART, QT, 6])
        mv = sb("mv", [PART, QT, 2])
        vpe, rst, nt1, nt2 = (sb(n, [PART, QT]) for n in ("vpe", "rst", "nt1", "nt2"))
        rr = sb("rr", [PART, QT])
        lg = sb("lg", [PART, QT, EXPERTS])
        eg = sb("eg", [PART, QT, EXPERTS])
        m8 = sb("m8", [PART, QT, 8])
        i8 = sb("i8", [PART, QT, 8], u32)
        i8f = sb("i8f", [PART, QT, 2])
        dm, tm, pr = sb("dm", [PART, QT]), sb("tm", [PART, QT]), sb("pr", [PART, QT, 2])
        nmg, sumg, rg = (sb(n, [PART, QT]) for n in ("nmg", "sumg", "rg"))
        oh = sb("oh", [PART, QT, 2, EXPERTS])
        weT = sb("weT", [EXPERTS, QT, PART])

        pA = [ctx.enter_context(nc.psum_tensor(f"pA{i}", [PART, BANK], fp32)) for i in range(3)]
        pB = [ctx.enter_context(nc.psum_tensor(f"pB{i}", [PART, 2 * BANK], fp32)) for i in range(2)]
        pO = ctx.enter_context(nc.psum_tensor("pO", [PART, BANK], fp32))

        kscr = [nc.dram_tensor(f"kscr{s}", (HEADS, 4, HD, CTX), fp16, kind="Internal").ap() for s in range(2)]
        qscr = [nc.dram_tensor(f"qscr{s}", (HEADS, 4, HD, SEQ), fp16, kind="Internal").ap() for s in range(2)]

        first_in = sem("first_in")
        w_in = sem("w_in")
        we_in = sem("we_in")
        w1_in = [sem(f"w1_in{n}") for n in range(len(SPLITS) - 1)]
        hi_ready = sem("hi_ready")
        w_split, w_split_rest = sem("w_split"), sem("w_split_rest")
        pad_in = sem("pad_in")
        zeroed = sem("zeroed")
        x_in = [sem(f"x_in{s}") for s in range(2)]
        ctx_in = sem("ctx_in")
        side_in = [sem(f"side_in{k}") for k in range(2 * QT)]
        stage_in = [sem(f"stage_in{r}") for r in range(STAGES)]
        k_stored = sem("k_stored")
        q_stored = sem("q_stored")
        out_stored = [sem(f"out_stored{s}") for s in range(2)]
        a_full, a_done = sem("a_full"), sem("a_done")
        b_full, b_done = sem("b_full"), sem("b_done")
        pv_full, pv_done = sem("pv_full"), sem("pv_done")
        y_ready = sem("y_ready")
        var_ready, rstd_ready = sem("var_ready"), sem("rstd_ready")
        mw_ready = sem("mw_ready")
        side_scaled = sem("side_scaled")
        coef_ready = sem("coef_ready")
        nm1_ready, p1_ready = sem("nm1_ready"), sem("p1_ready")
        dm_ready, tm_ready = sem("dm_ready"), sem("tm_ready")
        nmg_ready, eg_ready = sem("nmg_ready"), sem("eg_ready")
        we_ready = sem("we_ready")
        x_final = sem("x_final")
        tgate_ready = sem("tgate_ready")
        chain = sem("chain")
        pool_chain = sem("pool_chain")
        passed, pool_passed, sp_passed = sem("passed"), sem("pool_passed"), sem("sp_passed")

        block = ctx.enter_context(nc.Block())

        x_v = io["x"].rearrange("(j s) (q p) d -> j s p q d", s=2, p=PART)
        out_v = out.rearrange("(j s) (q p) d -> j s p q d", s=2, p=PART)
        ctx_v = io["ctxT"].rearrange("(j s) d t -> j s d t", s=2)
        side_v = io["side"].rearrange("(j s) (q p) t -> j s q p t", s=2, p=PART)

        def at(view, it, *rest):
            if isinstance(it, int):
                return view[(it, *rest)]
            return view[bass.ds(it, 1)][(0, *rest)]

        def split_source(n, e, name):
            if name == "wg":
                return wg[:, :]
            if name == "rw1":
                return probs[0][:, 0:HID]
            return (sc1 + [h[:, :, :].rearrange("p c q -> p (c q)") for h in hid])[n - 1][:, e * HID:(e + 1) * HID]

        def split_half(w, name, half):
            return wg16[half][:, :] if name == "wg" else rw1[half][:, :] if name == "rw1" else w1[int(name[-1])][half][:, w, :]

        def wait_split(eng):
            eng.wait_ge(w_split, WEIGHTS_FIRST)
            eng.wait_ge(w_split_rest, len(SPLITS) - WEIGHTS_FIRST)

        def both(body, eng):
            with eng.Fori(0, PAIRS - 1) as j:
                body(j, PAIR)
            body(PAIRS - 1, LAST)

        @block.sync
        def _(sp):
            def load(dst, src, s):
                sp.dma_start(dst, src).then_inc(s, 16)

            def load_x(j, s):
                load(xin[s][:, :, :], at(x_v, j, s), x_in[s])

            def load_ctx(j, s):
                load(ctxT[:, :], at(ctx_v, j, s), ctx_in)

            def store_k(s, plan, base):
                sp.wait_ge(a_done, base + plan.at["A", ("keys0", s, len(CHUNKS) - 1)])
                sp.sem_inc(sp_passed, 1)
                for p, src in ((1, khi), (2, klo), (3, khi)):
                    sp.dma_start(kscr[s][:, p, :, :], src).then_inc(k_stored, 16)

            def store_q(s, plan, base):
                sp.wait_ge(a_done, base + plan.at["A", ("query0", s)])
                sp.sem_inc(sp_passed, 1)
                for p, src in ((1, qhi), (2, qhi), (3, qlo)):
                    sp.dma_start(qscr[s][:, p, :, :], src[:, :]).then_inc(q_stored, 16)

            def stage(i, j):
                s, g, r = i // GROUPS % 2, i % GROUPS, i % STAGES
                if g == 0:
                    sp.wait_ge(k_stored, 48 * (2 * j + i // GROUPS + 1))
                    sp.sem_inc(sp_passed, 1)
                    sp.wait_ge(q_stored, 48 * (2 * j + i // GROUPS + 1))
                    sp.sem_inc(sp_passed, 1)
                if i >= STAGES:
                    sp.wait_ge(b_full, before("B", j) + PAIR.at["B", ("s2", i - STAGES, KT - 1)])
                    sp.sem_inc(sp_passed, 1)
                sp.dma_start(kst[r][:, :], kscr[s][g * GH:(g + 1) * GH].rearrange("h p c t -> (h p c) t"))\
                    .then_inc(stage_in[r], 16)
                for h in range(GH):
                    sp.dma_start(qst[r][ROWS * h:ROWS * (h + 1), h, :],
                                 qscr[s][g * GH + h].rearrange("p c q -> (p c) q")).then_inc(stage_in[r], 16)

            def load_hidden(n):
                for e, (w, name) in enumerate(SPLITS[n]):
                    load(split_source(n, e, name), io[name] if w is None else io[name][:, w, :], w1_in[n])

            load_ctx(0, 0)
            for dst, name in ((wk0, "wk0"), (bcol, "bcol"), (wk1, "wk1"), (wv, "wv")):
                load(dst[:, :], io[name], first_in)
            load_x(0, 0)
            for dst, name in ((ident, "ident"), (wq0, "wq0"), (bv1, "bv1"), (iota, "iota"), (wo0, "wo0"),
                              (wq1, "wq1"), (bo, "bo"), (gates, "gates"), (rb1, "rb1"), (rb2, "rb2"), (wg, "wg")):
                load(dst[:, :], io[name], w_in)
            load(betas[:, 0:3], io["betas"], w_in)
            load(rw2[:, :, :], io["rw2"], w_in)
            for s in range(2):
                sp.dma_start(kscr[s][:, 0, :, :], io["kpad"]).then_inc(pad_in, 16)
                sp.dma_start(qscr[s][:, 0, :, :], io["qpad"]).then_inc(pad_in, 16)
                sp.sem_inc(out_stored[s], 16)
            load_x(0, 1)
            for n in range(WEIGHTS_FIRST):
                load_hidden(n)
            sp.wait_ge(pad_in, 64)
            sp.wait_ge(zeroed, 2)
            store_k(0, PROLOGUE, 0)
            sp.wait_ge(b_full, PROLOGUE.at["B", ("values", 0, LAST_VALUES)])
            load_ctx(0, 1)
            store_q(0, PROLOGUE, 0)
            for i in range(STAGES):
                stage(i, 0)
            for n in range(WEIGHTS_FIRST, len(SPLITS) - 1):
                load_hidden(n)
            for l in range(2):
                load(w2[l][:, :, :, :], io[f"w2_{l}"], we_in)
                load(b1[l][:, :, :], io[f"b1_{l}"], we_in)
                load(b2[l][:, :], io[f"b2_{l}"], we_in)

            def body(j, plan):
                more = plan is PAIR
                base = before("A", j)
                sp.wait_ge(a_full, base)
                sp.sem_inc(sp_passed, 1)
                wait_split(sp)
                for k in range(2 * QT):
                    load(sc1[k][:, :], at(side_v, j, k // QT, k % QT), side_in[k])
                store_k(1, plan, base)
                store_q(1, plan, base)
                if more:
                    sp.wait_ge(b_full, before("B", j) + plan.at["B", ("values", 1, LAST_VALUES)])
                    sp.sem_inc(sp_passed, 1)
                    load_ctx(j + 1, 0)
                for i in range(STAGES, NG):
                    stage(i, j)
                if more:
                    for s in range(2):
                        sp.wait_ge(y_ready, before("finish", j) + plan.at["finish", ("finish", s, "m0")])
                        sp.sem_inc(sp_passed, 1)
                        load_x(j + 1, s)
                    store_k(0, plan, base)
                    sp.wait_ge(b_full, before("B", j) + plan.at["B", ("values", 0, LAST_VALUES)])
                    sp.sem_inc(sp_passed, 1)
                    load_ctx(j + 1, 1)
                    store_q(0, plan, base)
                    for i in range(NG, NG + STAGES):
                        stage(i, j)
                for s in range(2):
                    sp.wait_ge(x_final, 2 * j + s + 1)
                    sp.sem_inc(sp_passed, 1)
                    sp.dma_start(at(out_v, j, s), xres[s][:, :, :]).then_inc(out_stored[s], 16)

            both(body, sp)
            for s in range(2):
                sp.wait_ge(out_stored[s], 16 * (PAIRS + 1))

        @block.gpsimd
        def _(pool):
            pool.memset(neghalf[:, :], -0.5).then_inc(zeroed, 1)
            pool.wait_ge(zeroed, 1)

            def run(plan, j):
                for kind, *a in plan.steps:
                    if kind == "norm":
                        pool.wait_ge(var_ready, before("norm", j, plan) + plan.at["norm", (kind, *a)])
                        pool.tensor_tensor(rst[:, :], vpe[:, :], neghalf[:, :], ALU.pow).then_inc(rstd_ready, 1)
                    elif kind == "scale_side":
                        k, = a
                        pool.wait_ge(side_in[k], 16 * (j + 1))
                        pool.sem_inc(pool_passed, 1)
                        pool.tensor_scalar(sc1[k][:, :], sc1[k][:, :], betas[:, 3:4], 0.0, ALU.mult, ALU.add)\
                            .then_inc(side_scaled, 1)

            run(PROLOGUE, 0)
            for n in range(WEIGHTS_FIRST, len(SPLITS)):
                pool.wait_ge(hi_ready, n + 1)
                for e, (w, name) in enumerate(SPLITS[n]):
                    src = split_source(n, e, name)
                    pool.tensor_scalar(src, src, W_SCALE, None, ALU.mult).then_inc(pool_chain, 1)
                    pool.wait_ge(pool_chain, sum(len(x) for x in SPLITS[WEIGHTS_FIRST:n]) + e + 1)
                    last = pool.tensor_tensor(split_half(w, name, 1), src, split_half(w, name, 0), ALU.subtract)
                last.then_inc(w_split_rest, 1)
            pool.wait_ge(coef_ready, 1)
            both(lambda j, plan: run(plan, j), pool)

        @block.scalar
        def _(act):
            act.wait_ge(first_in, 16 * 4)

            def upper_halves(n):
                if n < len(SPLITS) - 1:
                    act.wait_ge(w1_in[n], 16 * len(SPLITS[n]))
                for e, (w, name) in enumerate(SPLITS[n]):
                    last = act.activation(split_half(w, name, 0), split_source(n, e, name), ACT.Identity, scale=W_SCALE)
                last.then_inc(hi_ready, 1)

            def run(plan, j):
                def next_b(step):
                    n = plan.unit("B", step)
                    act.wait_ge(b_full, before("B", j, plan) + n)
                    return pB[(n - 1) % 2]

                for kind, *a in plan.steps:
                    if kind == "keys1":
                        s, h = a
                        c0 = 2 * BANK * h
                        w = min(2 * BANK, CTX - c0)
                        banks = next_b((kind, *a))
                        act.activation(k1T[s][:, c0:c0 + w], banks[:, 0:w], ACT.Identity, bias=bcol[:, 3:4])\
                            .then_inc(b_done, 1)
                    elif kind == "values":
                        s, t0 = a
                        banks = next_b((kind, *a))
                        m = min(4, KT - t0)
                        kr = tile_rows(t0 + m - 1)
                        src = banks[0:kr, 0:m * 2 * DIM].rearrange("p (t v) -> p t v", t=m)
                        act.activation(v1[s][0:kr, t0:t0 + m, :], src[:, :, DIM:2 * DIM], ACT.Identity)
                        act.activation(vst[s][0:kr, t0:t0 + m, :, 0:HD],
                                       src[:, :, 0:DIM].rearrange("p t (h c) -> p t h c", c=HD), ACT.Identity)\
                            .then_inc(b_done, 1)
                    elif kind == "s2":
                        i, t = a
                        n, kr = i * KT + t, tile_rows(t)
                        banks = next_b((kind, *a))
                        act.activation(probs[n % 2][0:kr, :], banks[0:kr, :], ACT.Exp, scale=HD ** -0.5)\
                            .then_inc(b_done, 1)
                    elif kind == "up":
                        l, s, e, c = a
                        if c < HC - 1:
                            continue
                        if e == hidden(l, 0)[0][2] and l == s == 0:
                            act.wait_ge(we_in, 16 * 6)
                            wait_split(act)
                        r = hidden(l, 0).index((l, 0, e)) + s * len(hidden(l, 0))
                        banks = next_b((kind, *a))
                        for c in range(HC):
                            last = act.activation(hid[r % 2][:, c, :], banks[:, c * SEQ:(c + 1) * SEQ],
                                                  ACT.Silu if l == 0 else ACT.Gelu, scale=UNSCALE,
                                                  bias=rb1[:, c:c + 1] if e < 0 else b1[l][:, e, c:c + 1])
                        last.then_inc(b_done, 1)
                    elif kind == "tanh":
                        act.wait_ge(dm_ready, 2 * j + a[0] + 1)
                        act.activation(tm[:, :], dm[:, :], ACT.Tanh, scale=0.5).then_inc(tm_ready, 1)
                    elif kind == "exp1":
                        k, = a
                        act.wait_ge(nm1_ready, 2 * QT * j + k + 1)
                        act.activation(sc1[k][:, :], sc1[k][:, :], ACT.Exp, bias=nm1[:, k:k + 1],
                                       accum_out=sum1[:, k:k + 1]).then_inc(p1_ready, 1)
                    elif kind == "split":
                        upper_halves(a[0])
                    elif kind == "exp_gate":
                        act.wait_ge(nmg_ready, 2 * j + a[0] + 1)
                        for r in range(QT):
                            last = act.activation(eg[:, r, :], lg[:, r, :], ACT.Exp, bias=nmg[:, r:r + 1],
                                                  accum_out=sumg[:, r:r + 1])
                        last.then_inc(eg_ready, 1)

            run(PROLOGUE, 0)
            act.wait_ge(w_in, 16 * 13)
            act.activation(tgate[:, :], gates[:, :], ACT.Tanh).then_inc(tgate_ready, 1)
            for n in range(WEIGHTS_FIRST, len(SPLITS)):
                upper_halves(n)
            act.wait_ge(w_split, 1)
            both(lambda j, plan: run(plan, j), act)

        @block.tensor
        def _(pe):
            mm, turn = nc.tensor.matmul, nc.tensor.transpose

            def run(plan, j):
                base_a, base_b = before("A", j, plan), before("B", j, plan)

                def open_a():
                    n = plan.unit("A", step)
                    pe.wait_ge(a_done, free_at(base_a, n, 3))
                    return pA[(n - 1) % 3]

                def open_b():
                    n = plan.unit("B", step)
                    pe.wait_ge(b_done, free_at(base_b, n, 2))
                    return pB[(n - 1) % 2]

                def turn_two(bank, src, rows=PART):
                    for r in range(QT):
                        last = turn(bank[0:rows, r * PART:(r + 1) * PART], src(r), ident[:, :])
                    last.then_inc(a_full, 1)

                for step in plan.steps:
                    kind, *a = step
                    if kind == "keys0":
                        s, c = a
                        c0, w = CHUNKS[c]
                        bank = open_a()
                        if c == 0:
                            pe.wait_ge(ctx_in, 16 * (slot_number(plan, j, s) + 1))
                        mm(bank[:, 0:w], wk0[:, :], ctxT[:, c0:c0 + w], start=True, stop=True).then_inc(a_full, 1)
                    elif kind == "keys1":
                        s, h = a
                        c0 = 2 * BANK * h
                        banks = open_b()
                        for o in range(0, min(2 * BANK, CTX - c0), BANK):
                            m = min(BANK, CTX - c0 - o)
                            last = mm(banks[:, o:o + m], wk1[:, :], ctxT[:, c0 + o:c0 + o + m], start=True, stop=True)
                        last.then_inc(b_full, 1)
                    elif kind == "values":
                        s, t0 = a
                        banks = open_b()
                        for t in range(t0, min(t0 + 4, KT)):
                            kr = tile_rows(t)
                            last = mm(banks[0:kr, (t - t0) * 2 * DIM:(t - t0 + 1) * 2 * DIM],
                                      ctxT[:, t * PART:t * PART + kr], wv[:, :], start=True, stop=True)
                        last.then_inc(b_full, 1)
                    elif kind == "turn":
                        s, what = a
                        bank = open_a()
                        if plan is PROLOGUE:
                            pe.wait_ge(w_in, 16 * 13)
                        pe.wait_ge(y_ready, before("finish", j, plan) + plan.at["finish", ("finish", s, what)])
                        turn_two(bank, lambda r: y["q" if what == "q" else "x"][:, r, :])
                    elif kind in ("query0", "query1"):
                        s, = a
                        bank = open_a()
                        pe.wait_ge(a_done, base_a + plan.at["A", ("turn", s, "q" if kind == "query0" else "a1")])
                        w, src = (wq0, yT["q"]) if kind == "query0" else (wq1, yT[s])
                        mm(bank[:, 0:SEQ], w[:, :], src[:, :], start=True, stop=True).then_inc(a_full, 1)
                    elif kind == "s1":
                        i, u, c = a
                        c0, w = CHUNKS[c]
                        h, r, st = u // QT, u % QT, i % STAGES
                        bank = open_a()
                        if u == 0 and c == 0:
                            pe.wait_ge(stage_in[st], 16 * (1 + GH) * (2 * j + i // STAGES + 1))
                        mm(bank[:, 0:w], qst[st][:, h, r * PART:(r + 1) * PART], kst[st][:, c0:c0 + w],
                           start=True, stop=True).then_inc(a_full, 1)
                    elif kind == "put_max":
                        bank = open_a()
                        pe.wait_ge(mw_ready, before("split_max", j, plan) + plan.at["split_max", ("split_max", a[0])])
                        turn_two(bank, lambda r: mw[:, r, :])
                    elif kind == "s2":
                        i, t = a
                        kr, st = tile_rows(t), i % STAGES
                        banks = open_b()
                        if t == 0:
                            pe.wait_ge(a_done, base_a + (plan.at["A", ("put_max", i)] if i >= PRE else 0))
                        for h in range(0, GH, 2):
                            last = mm(banks[0:kr, h * SEQ:(h + 2) * SEQ], kst[st][:, t * PART:t * PART + kr],
                                      qst[st][:, h:h + 2, :], start=True, stop=True)
                        last.then_inc(b_full, 1)
                    elif kind == "weigh":
                        i, t = a
                        n, kr, s = i * KT + t, tile_rows(t), i // GROUPS
                        if t == 0:
                            pe.wait_ge(pv_done, NG * j + i + 1)
                        pe.wait_ge(b_done, base_b + plan.at["B", ("s2", i, t)])
                        for h in range(GH):
                            last = mm(pO[ROWS * h:ROWS * h + HD + 1, 0:SEQ], vst[s][0:kr, t, (i % GROUPS) * GH + h, :],
                                      probs[n % 2][0:kr, h * SEQ:(h + 1) * SEQ], start=(t == 0), stop=(t == KT - 1))
                        if t == KT - 1:
                            last.then_inc(pv_full, 1)
                    elif kind == "turn_out":
                        bank = open_a()
                        pe.wait_ge(pv_done, NG * j + a[0] + 2)
                        turn_two(bank, lambda r: oTs[:, r * PART:(r + 1) * PART])
                    elif kind == "turn_attn":
                        s, = a
                        bank = open_a()
                        pe.wait_ge(a_done, base_a + plan.at["A", ("turn_out", GROUPS * (s + 1) - 1)])
                        turn_two(bank, lambda r: attn[:, r, :])
                    elif kind == "project":
                        bank = open_a()
                        pe.wait_ge(a_done, base_a + plan.at["A", ("turn_attn", a[0])])
                        for r in range(QT):
                            last = mm(bank[:, r * DIM:(r + 1) * DIM], attnT[:, r * PART:(r + 1) * PART], wo0[:, :],
                                      start=True, stop=True)
                        last.then_inc(a_full, 1)
                    elif kind == "up":
                        l, s, e, c = a
                        if c == 0:
                            banks_up = open_b()
                            if (l, s, e) == hidden(l, s)[0]:
                                pe.wait_ge(a_done, base_a + plan.at["A", ("turn", s, f"m{l}")])
                                if l == s == 0:
                                    wait_split(pe)
                        for n, (wh, yh) in enumerate(HALVES):
                            w = rw1[wh][:, c * PART:(c + 1) * PART] if e < 0 else w1[l][wh][:, e, c * PART:(c + 1) * PART]
                            last = mm(banks_up[:, c * SEQ:(c + 1) * SEQ], w, y16[s][yh], start=(n == 0), stop=(n == 2))
                        if c == HC - 1:
                            last.then_inc(b_full, 1)
                    elif kind == "down":
                        l, s, e = a
                        h = hid[(hidden(l, 0).index((l, 0, e)) + s * len(hidden(l, 0))) % 2]
                        bank = open_a()
                        if (l, s, e) == hidden(0, 0)[0]:
                            pe.wait_ge(we_in, 16 * 6)
                        pe.wait_ge(b_done, base_b + plan.unit("B", ("up", l, s, e, 0)))
                        n = EXPERTS if e < 0 else DIM
                        for r in range(QT):
                            for c in range(HC):
                                last = mm(bank[:, r * n:(r + 1) * n], h[:, c, r * PART:(r + 1) * PART],
                                          rw2[:, c, :] if e < 0 else w2[l][:, e, c, :], start=(c == 0), stop=(c == HC - 1))
                        last.then_inc(a_full, 1)
                    elif kind == "gate":
                        s, = a
                        bank = open_a()
                        pe.wait_ge(a_done, base_a + plan.at["A", ("turn", s, "m1")])
                        for r in range(QT):
                            for n, (wh, yh) in enumerate(HALVES):
                                last = mm(bank[:, r * EXPERTS:(r + 1) * EXPERTS], y16[s][yh][:, r * PART:(r + 1) * PART],
                                          wg16[wh][:, :], start=(n == 0), stop=(n == 2))
                        last.then_inc(a_full, 1)
                    elif kind == "turn_we":
                        l, s = a
                        bank = open_a()
                        pe.wait_ge(we_ready, 4 * j + 2 * l + s + 1)
                        turn_two(bank, lambda r: we[s][:, r, :], EXPERTS)
                    elif kind == "bias2":
                        l, s = a
                        bank = open_a()
                        pe.wait_ge(a_done, base_a + plan.at["A", ("turn_we", l, s)])
                        for r in range(QT):
                            last = mm(bank[:, r * DIM:(r + 1) * DIM], weT[:, r, :], b2[l][:, :], start=True, stop=True)
                        last.then_inc(a_full, 1)
                    elif kind == "qk":
                        k, c = a
                        c0, w = CHUNKS[c]
                        bank = open_a()
                        if c == 0:
                            pe.wait_ge(a_done, base_a + plan.at["A", ("query1", k // QT)])
                        mm(bank[:, 0:w], q1T[:, k % QT * PART:(k % QT + 1) * PART], k1T[k // QT][:, c0:c0 + w],
                           start=True, stop=True).then_inc(a_full, 1)
                    elif kind == "turn_p":
                        k, b = a
                        if b == 0:
                            pe.wait_ge(p1_ready, 2 * QT * j + k + 1)
                        bank = open_a()
                        for t in range(4 * b, min(4 * b + 4, KT)):
                            kr = tile_rows(t)
                            last = turn(bank[0:kr, t % 4 * PART:(t % 4 + 1) * PART], sc1[k][:, t * PART:t * PART + kr],
                                        ident[:, :])
                        last.then_inc(a_full, 1)
                    elif kind == "out1":
                        k, = a
                        bank = open_a()
                        pe.wait_ge(a_done, base_a + plan.at["A", ("turn_p", k, (KT - 1) // 4)])
                        for t in range(KT):
                            kr = tile_rows(t)
                            last = mm(bank[:, 0:DIM], p1T[0:kr, t, :], v1[k // QT][0:kr, t, :],
                                      start=(t == 0), stop=(t == KT - 1))
                        last.then_inc(a_full, 1)

            pe.wait_ge(first_in, 16 * 4)
            run(PROLOGUE, 0)
            both(lambda j, plan: run(plan, j), pe)

        @block.vector
        def _(dve):
            v = nc.vector

            def run(plan, j):
                base_a = before("A", j, plan)
                links = [0 if plan is PROLOGUE else 2 + before("links", j), 0]
                taken = [0]
                mw_of = mw[:, :, :].rearrange("p q (h r) -> p h q r", h=GH)

                def link(ins, alone=False):
                    links[1] += 1
                    ins.then_inc(chain, 1)
                    dve.wait_ge(chain, links[0] + links[1])
                    if alone:
                        dve.sem_inc(passed, 1)

                def next_a(alone=False):
                    taken[0] = n = plan.unit("A", step)
                    dve.wait_ge(a_full, base_a + n)
                    if alone:
                        dve.sem_inc(passed, 1)
                    return pA[(n - 1) % 3]

                def done():
                    return base_a + taken[0]

                def top_two(l, s):
                    for r in range(QT):
                        last = v.max(m8[:, r, :], lg[:, r, :])
                    link(last)
                    if l == 0:
                        v.tensor_tensor(dm[:, :], m8[:, :, 0], m8[:, :, 1], ALU.subtract).then_inc(dm_ready, 1)
                    else:
                        v.tensor_scalar(nmg[:, :], m8[:, :, 0], -1.0, None, ALU.mult).then_inc(nmg_ready, 1)
                    for r in range(QT):
                        last = v.max_index(i8[:, r, :], m8[:, r, :], lg[:, r, :])
                    link(last)
                    link(v.tensor_copy(i8f[:, :, :], i8[:, :, 0:2]))

                def weights_of_two(l, s):
                    if l == 0:
                        dve.wait_ge(tm_ready, 2 * j + s + 1)
                        v.tensor_scalar(pr[:, :, 0], tm[:, :], 0.5, 0.5, ALU.mult, ALU.add)
                        link(v.tensor_scalar(pr[:, :, 1], tm[:, :], -0.5, 0.5, ALU.mult, ALU.add))
                    else:
                        dve.wait_ge(eg_ready, 2 * j + s + 1)
                        link(v.reciprocal(rg[:, :], sumg[:, :]))
                    for r in range(QT):
                        for k in range(2):
                            w = pr[:, r, k:k + 1] if l == 0 else rg[:, r:r + 1]
                            last = v.tensor_scalar(oh[:, r, k, :], iota[:, :], i8f[:, r, k:k + 1], w,
                                                   ALU.is_equal, ALU.mult)
                    link(last)
                    if l == 0:
                        v.tensor_tensor(we[s][:, :, :], oh[:, :, 0, :], oh[:, :, 1, :], ALU.add).then_inc(we_ready, 1)
                    else:
                        link(v.tensor_tensor(oh[:, :, 0, :], oh[:, :, 0, :], oh[:, :, 1, :], ALU.add))
                        v.tensor_tensor(we[s][:, :, :], oh[:, :, 0, :], eg[:, :, :], ALU.mult).then_inc(we_ready, 1)

                for step in plan.steps:
                    kind, *a = step
                    if kind == "keys0":
                        s, c = a
                        c0, w = CHUNKS[c]
                        bank = next_a()
                        if c == 0 and plan is not PROLOGUE:
                            dve.wait_ge(k_stored, 48 * slot_number(plan, j, s))
                        link(v.tensor_scalar(khi[:, c0:c0 + w], bank[:, 0:w], bcol[:, 1:2], None, ALU.add))
                        v.scalar_tensor_tensor(klo[:, c0:c0 + w], bank[:, 0:w], bcol[:, 1:2], khi[:, c0:c0 + w],
                                               op0=ALU.add, op1=ALU.subtract).then_inc(a_done, 1)
                    elif kind == "norm":
                        s, what = a
                        src = xin[s] if what == "q" else xres[s]
                        if what == "q":
                            dve.wait_ge(x_in[s], 16 if plan is PROLOGUE else 16 * (j + 2 - s))
                        for r in range(QT):
                            last = v.bn_stats(bst[:, r, :], src[:, r, :])
                        link(last, alone=True)
                        for r in range(QT):
                            last = v.bn_aggr(mv[:, r, :], bst[:, r, :])
                        link(last)
                        v.tensor_scalar(vpe[:, :], mv[:, :, 1], EPS, None, ALU.add).then_inc(var_ready, 1)
                    elif kind == "finish":
                        s, what = a
                        src = xin[s] if what == "q" else xres[s]
                        dst = y["q" if what == "q" else "x"]
                        dve.wait_ge(rstd_ready, before("finish", j, plan) + plan.at["finish", step])
                        link(v.tensor_tensor(nt1[:, :], rst[:, :], rst[:, :], ALU.mult))
                        link(v.tensor_tensor(nt2[:, :], nt1[:, :], vpe[:, :], ALU.mult))
                        link(v.tensor_scalar(nt1[:, :], nt2[:, :], -0.5, 1.5, ALU.mult, ALU.add))
                        link(v.tensor_tensor(rr[:, :], nt1[:, :], rst[:, :], ALU.mult))
                        for r in range(QT):
                            last = v.tensor_scalar(dst[:, r, :], src[:, r, :], mv[:, r, 0:1], rr[:, r:r + 1],
                                                   ALU.subtract, ALU.mult)
                        last.then_inc(y_ready, 1)
                    elif kind == "turn":
                        s, what = a
                        bank = next_a()
                        if what in ("m0", "m1"):
                            link(v.tensor_scalar(y16[s][0], bank[:, 0:SEQ], Y_SCALE, None, ALU.mult))
                            v.scalar_tensor_tensor(y16[s][1], bank[:, 0:SEQ], Y_SCALE, y16[s][0],
                                                   op0=ALU.mult, op1=ALU.subtract).then_inc(a_done, 1)
                        else:
                            v.tensor_copy(yT["q" if what == "q" else s][:, :], bank[:, 0:SEQ]).then_inc(a_done, 1)
                    elif kind == "query0":
                        s, = a
                        bank = next_a()
                        if plan is not PROLOGUE:
                            dve.wait_ge(q_stored, 48 * slot_number(plan, j, s))
                        link(v.tensor_scalar(qhi[:, :], bank[:, 0:SEQ], bcol[:, 0:1], None, ALU.add))
                        v.scalar_tensor_tensor(qlo[:, :], bank[:, 0:SEQ], bcol[:, 0:1], qhi[:, :],
                                               op0=ALU.add, op1=ALU.subtract).then_inc(a_done, 1)
                    elif kind == "s1":
                        i, u, c = a
                        bank = next_a()
                        v.reduce_max(mxp[:, u, c:c + 1], bank[:, 0:CHUNKS[c][1]], axis=AX.X).then_inc(a_done, 1)
                    elif kind == "split_max":
                        dve.wait_ge(a_done, done())
                        link(v.tensor_reduce(mw_of[:, :, :, 0], mxp[:, :, :].rearrange("p (h q) c -> p h q c", h=GH),
                                             axis=AX.X, op=ALU.max, negate=True))
                        link(v.tensor_scalar(m16[:, :, :], mw_of[:, :, :, 0], 1 / MAX_SCALE, None, ALU.mult))
                        v.scalar_tensor_tensor(mw_of[:, :, :, 1], m16[:, :, :], -MAX_SCALE, mw_of[:, :, :, 0],
                                               op0=ALU.mult, op1=ALU.add).then_inc(mw_ready, 1)
                    elif kind == "put_max":
                        i, = a
                        bank = next_a()
                        for h in range(GH):
                            p = ROWS * h
                            last = v.tensor_scalar(qst[i % STAGES][p:p + 2, h, :], bank[p:p + 2, 0:SEQ],
                                                   1 / MAX_SCALE, None, ALU.mult)
                        last.then_inc(a_done, 1)
                    elif kind == "keep_out":
                        dve.wait_ge(pv_full, NG * j + a[0] + 1)
                        v.tensor_copy(oTs[:, :], pO[:, 0:SEQ]).then_inc(pv_done, 1)
                    elif kind == "turn_out":
                        g = a[0] % GROUPS
                        bank = next_a()
                        o = bank[:, 0:SEQ].rearrange("p (q h r) -> p q h r", q=QT, h=GH)
                        link(v.reciprocal(rec[:, :, :], o[:, :, :, HD]))
                        dst = attn[:, :, g * GH * HD:(g + 1) * GH * HD].rearrange("p q (h c) -> p q h c", c=HD)
                        v.tensor_tensor(dst, o[:, :, :, 0:HD], rec[:, :, :].unsqueeze(3).broadcast_to([PART, QT, GH, HD]),
                                        ALU.mult).then_inc(a_done, 1)
                    elif kind == "turn_attn":
                        bank = next_a()
                        v.tensor_scalar(attnT[:, :], bank[:, 0:SEQ], bcol[:, 4:5], None, ALU.add).then_inc(a_done, 1)
                    elif kind == "project":
                        s, = a
                        bank = next_a()
                        for r in range(QT):
                            last = v.tensor_tensor(oproj[:, r, :], bank[:, r * DIM:(r + 1) * DIM], bo[:, :], ALU.add)
                        last.then_inc(a_done, 1)
                        dve.wait_ge(a_done, done())
                        dve.wait_ge(out_stored[s], 16 * (j + 1))
                        link(v.scalar_tensor_tensor(xres[s][:, :, :], oproj[:, :, :], tgate[:, 0:1], xin[s][:, :, :],
                                                    op0=ALU.mult, op1=ALU.add))
                    elif kind in ("down", "gate") and (kind == "gate" or a[2] < 0):
                        l, s = (1, a[0]) if kind == "gate" else (0, a[1])
                        bank = next_a()
                        for r in range(QT):
                            src = bank[:, r * EXPERTS:(r + 1) * EXPERTS]
                            last = (v.tensor_tensor(lg[:, r, :], src, rb2[:, :], ALU.add) if l == 0
                                    else v.tensor_scalar(lg[:, r, :], src, UNSCALE, None, ALU.mult))
                        last.then_inc(a_done, 1)
                        dve.wait_ge(a_done, done())
                        dve.sem_inc(passed, 1)
                        top_two(l, s)
                    elif kind == "split":
                        n, = a
                        dve.wait_ge(hi_ready, n + 1)
                        for e, (w, name) in enumerate(SPLITS[n]):
                            last = v.scalar_tensor_tensor(split_half(w, name, 1), split_source(n, e, name), W_SCALE,
                                                          split_half(w, name, 0), op0=ALU.mult, op1=ALU.subtract)
                        last.then_inc(w_split, 1)
                    elif kind == "pick":
                        weights_of_two(*a)
                    elif kind == "down":
                        l, s, e = a
                        bank = next_a()
                        if e == 0:
                            dve.wait_ge(we_ready, 4 * j + 2 * l + s + 1)
                        else:
                            dve.wait_ge(a_done, base_a + plan.at["A", ("down", l, s, e - 1)])
                        for r in range(QT):
                            src = bank[:, r * DIM:(r + 1) * DIM]
                            if e == 0:
                                last = v.tensor_scalar(acc[s][:, r, :], src, we[s][:, r, e:e + 1], None, ALU.mult)
                            else:
                                last = v.scalar_tensor_tensor(acc[s][:, r, :], src, we[s][:, r, e:e + 1],
                                                              acc[s][:, r, :], op0=ALU.mult, op1=ALU.add)
                        last.then_inc(a_done, 1)
                    elif kind == "turn_we":
                        bank = next_a()
                        v.tensor_copy(weT[:, :, :], bank[0:EXPERTS, 0:SEQ].rearrange("e (q p) -> e q p", q=QT))\
                            .then_inc(a_done, 1)
                    elif kind == "bias2":
                        l, s = a
                        bank = next_a()
                        dve.wait_ge(a_done, base_a + plan.at["A", ("down", l, s, EXPERTS - 1)])
                        v.tensor_tensor(acc[s][:, :, :], bank[:, 0:QT * DIM].rearrange("p (q d) -> p q d", q=QT),
                                        acc[s][:, :, :], ALU.add).then_inc(a_done, 1)
                        dve.wait_ge(a_done, done())
                        ins = v.scalar_tensor_tensor(xres[s][:, :, :], acc[s][:, :, :], tgate[:, 2 + l:3 + l],
                                                     xres[s][:, :, :], op0=ALU.mult, op1=ALU.add)
                        if l == 0:
                            link(ins)
                        else:
                            ins.then_inc(x_final, 1)
                    elif kind == "query1":
                        s, = a
                        link(v.tensor_tensor(xres[s][:, :, :], xres[s][:, :, :],
                                             bv1[:, :].unsqueeze(1).broadcast_to([PART, QT, DIM]), ALU.add))
                        bank = next_a()
                        v.tensor_scalar(q1T[:, :], bank[:, 0:SEQ], bcol[:, 2:3], DIM ** -0.5, ALU.add, ALU.mult)\
                            .then_inc(a_done, 1)
                    elif kind == "qk":
                        k, c = a
                        c0, w = CHUNKS[c]
                        if c == 0:
                            dve.wait_ge(side_scaled, 2 * QT * j + k + 1)
                            dve.sem_inc(passed, 1)
                        bank = next_a(alone=True)
                        v.tensor_tensor_reduce(out=sc1[k][:, c0:c0 + w], in0=bank[:, 0:w], in1=sc1[k][:, c0:c0 + w],
                                               scale=1.0, scalar=-3.0e38, op0=ALU.add, op1=ALU.max,
                                               accum_out=mx1[:, k, c:c + 1]).then_inc(a_done, 1)
                    elif kind == "max1":
                        k, = a
                        dve.wait_ge(a_done, done())
                        v.tensor_reduce(nm1[:, k:k + 1], mx1[:, k, :], axis=AX.X, op=ALU.max, negate=True)\
                            .then_inc(nm1_ready, 1)
                    elif kind == "turn_p":
                        k, b = a
                        t0 = 4 * b
                        m = min(4, KT - t0)
                        kr = tile_rows(t0 + m - 1)
                        bank = next_a()
                        if k == 0 and b == 0:
                            dve.wait_ge(k_stored, 48 * (2 * j + 2))
                        v.tensor_copy(p1T[0:kr, t0:t0 + m, :],
                                      bank[0:kr, 0:m * PART].rearrange("p (t q) -> p t q", t=m)).then_inc(a_done, 1)
                    elif kind == "out1":
                        k, = a
                        s, r = k // QT, k % QT
                        dve.wait_ge(p1_ready, 2 * QT * j + k + 1)
                        link(v.reciprocal(rs1[:, k:k + 1], sum1[:, k:k + 1]))
                        link(v.tensor_tensor(rs1[:, k:k + 1], rs1[:, k:k + 1], tgate[:, 1:2], ALU.mult))
                        bank = next_a()
                        v.scalar_tensor_tensor(xres[s][:, r, :], bank[:, 0:DIM], rs1[:, k:k + 1], xres[s][:, r, :],
                                               op0=ALU.mult, op1=ALU.add).then_inc(a_done, 1)
                        if r == QT - 1:
                            dve.wait_ge(a_done, done())
                assert links[1] == plan.count["links"], (links, plan.count["links"])

            v.memset(mw[:, :, :], 0.0)
            for r in range(STAGES):
                v.memset(qst[r][:, :, :].bitcast(fp32), 0.0)
            for s in range(2):
                v.memset(vst[s][:, :, :, :], 1.0)
            v.memset(pO[:, :], 0.0).then_inc(pv_done, 1)
            dve.wait_ge(pv_done, 1)
            v.memset(rec[:, :, :], 0.0).then_inc(zeroed, 1)
            dve.wait_ge(first_in, 16 * 4)
            dve.wait_ge(zeroed, 2)
            run(PROLOGUE, 0)
            dve.wait_ge(w_in, 16 * 13)
            v.tensor_tensor(betas[:, 3:4], betas[:, 0:1], betas[:, 1:2], ALU.add).then_inc(chain, 1)
            dve.wait_ge(chain, PROLOGUE.count["links"] + 1)
            v.tensor_tensor(betas[:, 3:4], betas[:, 3:4], betas[:, 2:3], ALU.subtract).then_inc(coef_ready, 1)
            dve.wait_ge(tgate_ready, 1)
            v.tensor_scalar(bv1[:, :], bv1[:, :], tgate[:, 1:2], None, ALU.mult).then_inc(chain, 1)
            dve.wait_ge(chain, PROLOGUE.count["links"] + 2)
            both(lambda j, plan: run(plan, j), dve)


def kernel(**inputs):
    import numpy as np
    import concourse.bacc as bacc
    from concourse import mybir as mb
    from concourse.bass_utils import run_bass_kernel_spmd as run

    a = {k: np.asarray(v) for k, v in inputs.items()}

    def col(*names):
        return np.stack([a[n].reshape(DIM) for n in names], 1)

    def row(v):
        return np.broadcast_to(v.reshape(1, -1), (PART, v.size))

    def chunked(v):
        return np.moveaxis(v.reshape(v.shape[:-1] + (HC, PART)), -1, 0)

    kpad = np.zeros((HEADS, HD, CTX), np.float16)
    kpad[:, 0:2] = MAX_SCALE
    io = {
        "x": a["x"], "side": a["fside_BxSxS2_0"], "ctxT": a["ctx_1024"].transpose(0, 2, 1),
        "ident": np.eye(PART, dtype=np.float32), "iota": row(np.arange(EXPERTS, dtype=np.float32)),
        "kpad": kpad, "qpad": np.zeros((HEADS, HD, SEQ), np.float16),
        "wk0": a["L0_xattn_Wk"], "wq0": a["L0_xattn_Wq"], "wo0": a["L0_xattn_Wo"],
        "wk1": a["L1_xattn_Wk"].T, "wq1": a["L1_xattn_Wq"].T,
        "wv": np.concatenate([a["L0_xattn_Wv"], a["L1_xattn_Wv"].T], 1),
        "bcol": col("L0_xattn_bq", "L0_xattn_bk", "L1_xattn_bq", "L1_xattn_bk", "L0_xattn_bv"),
        "bv1": row(a["L1_xattn_bv"]), "bo": row(a["L0_xattn_bo"]),
        "gates": row(np.concatenate([a["g_xattn"], a["g_ffn"]])),
        "betas": row(np.stack([a[f"L1_xattn_beta_{n}"].reshape(()) for n in ("risk", "prio", "impl")])),
        "rb1": chunked(a["L0_ffn_rb1"]), "rb2": row(a["L0_ffn_rb2"]), "rw1": a["L0_ffn_rw1"],
        "wg": a["L1_ffn_w_gate"].T, "rw2": a["L0_ffn_rw2"].reshape(HC, PART, EXPERTS).transpose(1, 0, 2),
    }
    for l, (n1, nb1, n2, nb2) in enumerate((("w1", "b1", "w2", "b2"), ("W1", "b1", "W2", "b2"))):
        io[f"w1_{l}"] = a[f"L{l}_ffn_{n1}"].transpose(1, 0, 2)
        io[f"b1_{l}"] = chunked(a[f"L{l}_ffn_{nb1}"])
        io[f"w2_{l}"] = a[f"L{l}_ffn_{n2}"].reshape(EXPERTS, HC, PART, DIM).transpose(2, 0, 1, 3)
        io[f"b2_{l}"] = a[f"L{l}_ffn_{nb2}"]

    nc = bacc.Bacc("TRN2", target_bir_lowering=False, num_devices=1)
    arrays, aps = {}, {}
    for name, v in io.items():
        v = np.ascontiguousarray(v)
        arrays[f"in_{name}"] = v
        aps[name] = nc.dram_tensor(f"in_{name}", v.shape, mb.dt.from_np(v.dtype), kind="ExternalInput").ap()
    out = nc.dram_tensor("out_0", (BATCH, SEQ, DIM), mb.dt.float32, kind="ExternalOutput").ap()
    flamingo(nc, aps, out)
    r = run(nc, [arrays], core_ids=[0])
    return r.results[0]["out_0"]
```

```python
import concourse.bass as bass
from concourse import mybir
from contextlib import ExitStack

BATCH, SEQ, CTX, DIM = 8, 256, 1601, 128
HEADS, HD = 16, 8
EXPERTS, HID = 8, 512
PART = 128
QT = SEQ // PART
KT = -(-CTX // PART)
HC = HID // PART
PAIRS = BATCH // 2
BANK = 512
CHUNKS = [(c, min(BANK, CTX - c)) for c in range(0, CTX, BANK)]
GH = 4
GROUPS = HEADS // GH
NG = 2 * GROUPS
ROWS = PART // GH
W_SCALE, Y_SCALE = 2.0 ** 8, 2.0 ** 11
UNSCALE = 1 / (W_SCALE * Y_SCALE)
HID_SCALE = (2.0 ** 4, 1.0)
HALVES = ((0, 0), (0, 1), (1, 0))
MAX_SCALE = 64.0
STAGES = 4
EPS = 1e-5

W1_COLS = 2 * EXPERTS * HID + HID + EXPERTS
W2_COLS = 2 * EXPERTS * HC * DIM + HC * EXPERTS
BUFFER_COLS = [3 * HID] * 4 + [2 * HID] * 3
SPLITS = [(k, sum(BUFFER_COLS[:b]), min(BUFFER_COLS[b], cols - sum(BUFFER_COLS[:b])), b)
          for k, cols in enumerate((W1_COLS, W2_COLS)) for b in range(len(BUFFER_COLS))]


def tile_rows(t):
    return min(PART, CTX - t * PART)


PUT_AFTER = 3
WEIGHTS_FIRST = 3
BY_POOL = (0, 2, 4, 6, 8, 10, 11)
PRE = 2




def prepare(s):
    keys = [("keys0", s, c) for c in range(len(CHUNKS))]
    return (keys[:2] + [("norm", s, "q")] + keys[2:] + [("finish", s, "q"), ("keys1", s, 0), ("turn", s, "q"), ("keys1", s, 1),
            ("query0", s)] + [("values", s, t) for t in range(0, KT, 4)])


def maxima(groups):
    steps = []
    for i in groups:
        chunks = []
        for half in range(2):
            chunks += [("s1", i, u, c) for u in range(GH * half, GH * (half + 1)) for c in range(len(CHUNKS) - 1)]
            chunks.append(("s1_rest", i, half))
        steps += chunks[:PUT_AFTER] + ([("put_max", i - 1)] if i > groups[0] else []) + chunks[PUT_AFTER:]
        steps.append(("split_max", i))
    return steps, [("put_max", groups[-1])]


def hidden(l, s):
    return [(l, s, e) for e in range(-1 if l == 0 else 0, EXPERTS)]


def hid_ring(l, s, e):
    return (hidden(l, 0) + hidden(l, 1)).index((l, s, e)) % 2


def halved_by_vector(l, s, e):
    return l == 0 or (s, e) == (1, EXPERTS - 1)


def weave(steps, fills):
    at = {}
    for first, last, more in fills:
        a, b = int(first * len(steps)), int(last * len(steps))
        for k, step in enumerate(more):
            at.setdefault(a + k * (b - a) // len(more), []).append(step)
    return [x for n, step in enumerate(steps) for x in [step] + at.get(n, [])]


def prologue():
    chunks, put = maxima(range(PRE))
    splits = [("split", n) for n in range(len(SPLITS))]
    first = prepare(0)
    return first[:5] + splits[:1] + first[5:] + splits[1:WEIGHTS_FIRST] + weave(chunks, [(0.15, 1.0, splits[WEIGHTS_FIRST:])]) + put


def attention0():
    steps = []
    for n in range(KT * NG):
        i, t = n // KT, n % KT
        steps.append(("s2", i, t))
        if t == 4 and i:
            steps.append(("turn_out", i - 1))
        if i == NG - 3 and t < 4:
            steps.append(("scale_side", t))
        if i == GROUPS:
            steps += {6: [("turn_attn", 0)], 7: [("project", 0)], 8: [("norm", 0, "m0")], 10: [("finish", 0, "m0")],
                      12: [("turn", 0, "m0")]}.get(t, [])
        if n > 1:
            steps.append(("weigh", (n - 2) // KT, (n - 2) % KT))
        if t == 1 and i:
            steps.append(("keep_out", i - 1))
    chunks, put = maxima(range(PRE, NG))
    return weave(steps, [(0.03, 0.2, prepare(1)), (0.0, 0.86, chunks + put)])


def down(ups, k):
    l, s, e = ups[k]
    return ([("pick", l, s)] if e == 0 else []) + [("down", l, s, e)] + ([("tanh", s)] if e < 0 else [])


def experts(ups, beside, before_down=()):
    steps = []
    for k, (l, s, e) in enumerate(ups):
        steps += [("up", l, s, e, c) for c in range(HC)]
        if k in before_down:
            steps += beside[k]
        if k:
            steps.append(("halve",) + ups[k - 1])
        if k > 1:
            steps += down(ups, k - 2)
        if k not in before_down:
            steps += beside.get(k, [])
    return steps + [("halve",) + ups[-1]] + down(ups, len(ups) - 2)


def pair(last):
    steps = attention0()
    coming = [] if last else prepare(0)
    queries = {step[0]: [step] for step in coming if step[0] in ("norm", "finish", "turn", "query0")}
    values = [step for step in coming if step[0] == "values"]
    keys = [step for step in coming if step[0] in ("keys0", "keys1")]

    ups = hidden(0, 0) + hidden(0, 1)
    steps += experts(ups, {
        0: [("weigh", NG - 1, KT - 2), ("weigh", NG - 1, KT - 1), ("keep_out", NG - 1)],
        1: [("turn_out", NG - 1)], 2: [("turn_attn", 1)],
        3: [("project", 1), ("norm", 1, "m0")], 4: [("finish", 1, "m0")], 6: [("turn", 1, "m0")],
        9: [("turn_we", 0, 0)], 10: [("bias2", 0, 0), ("norm", 0, "a1")], 11: [("finish", 0, "a1")],
        12: queries.get("norm", []), 13: [("turn", 0, "a1")] + queries.get("finish", []), 14: [("query1", 0)],
        15: [("qk", 0, c) for c in (0, 1)] + queries.get("turn", []) + [("turn_we", 0, 1)],
        16: [("qk", 0, c) for c in (2, 3)] + [("max1", 0)] + [("qk", 1, 0)],
        17: [("qk", 1, c) for c in (1, 2, 3)] + [("max1", 1)] + queries.get("query0", []),
    }, before_down=(9,))
    turns = lambda k: [("turn_p", k, b) for b in range(-(-KT // 4))]
    qk = lambda k: [("qk", k, c) for c in range(len(CHUNKS))] + [("max1", k)]
    part = [("exp1", 0), ("exp1", 1), ("down",) + ups[-1]] + turns(0)
    part += [("bias2", 0, 1), ("norm", 1, "a1"), ("out1", 0)] + turns(1)[:2] + [("finish", 1, "a1")] + turns(1)[2:]
    part += [("turn", 1, "a1"), ("out1", 1)]
    steps += weave(part, [(0.15, 1.0, keys)]) if keys else part
    part = [("query1", 1), ("norm", 0, "m1")] + qk(2)
    part += [("exp1", 2), ("finish", 0, "m1")] + qk(3) + [("exp1", 3), ("turn", 0, "m1")] + turns(2)
    part += [("gate", 0), ("out1", 2), ("exp_gate", 0)] + turns(3)
    steps += weave(part, [(0.0, 0.8, values)]) if values else part

    ups = hidden(1, 0) + hidden(1, 1)
    moe = experts(ups, {0: [("out1", 3), ("norm", 1, "m1")], 1: [("finish", 1, "m1")], 3: [("turn", 1, "m1")],
                        4: [("gate", 1), ("exp_gate", 1)],
                        8: [("turn_we", 1, 0)], 9: [("bias2", 1, 0)], 13: [("turn_we", 1, 1)]}, before_down=(8,))
    put = []
    if not last:
        chunks, put = maxima(range(NG, NG + PRE))
        moe = weave(moe, [(0.06, 1.0, chunks)])
    return steps + moe + [("down",) + ups[-1]] + put + [("bias2", 1, 1)]


LAST_VALUES = (KT - 1) // 4 * 4
ON_A = {"keys0", "turn", "query0", "s1", "s1_rest", "put_max", "turn_out", "turn_attn", "project", "down", "turn_we",
        "bias2", "query1", "qk", "turn_p", "out1", "gate"}
ON_B = {"keys1", "values", "s2", "up"}


class Plan:

    def __init__(self, steps):
        self.steps, self.count, self.at = steps, {}, {}
        for step in steps:
            if step[0] == "up" and step[-1] < HC - 1:
                continue
            for name in (["A"] if step[0] in ON_A else ["B"] if step[0] in ON_B else []) + [step[0]]:
                self.count[name] = self.count.get(name, 0) + 1
                self.at[name, step] = self.count[name]
        self.count["links"] = sum(LINKS.get(k, lambda *a: 0)(*a) for k, *a in steps)

    def unit(self, ring, step):
        return self.at[ring, ("up", *step[1:4], HC - 1) if step[0] == "up" else step]


LINKS = {"keys0": lambda *a: 1, "norm": lambda *a: 2, "finish": lambda *a: 4, "pick": lambda l, s: 4 if l else 3, "query0": lambda *a: 1, "query1": lambda *a: 1,
         "turn": lambda s, what: 1 if what in ("m0", "m1") else 0, "split_max": lambda *a: 2,
         "turn_out": lambda *a: 1, "project": lambda *a: 1, "down": lambda l, s, e: 3 if e < 0 else 0,
         "gate": lambda *a: 3, "bias2": lambda l, s: 1 if l == 0 else 0, "out1": lambda *a: 2}
PROLOGUE, PAIR, LAST = Plan(prologue()), Plan(pair(False)), Plan(pair(True))


def before(name, j, plan=PAIR):
    if plan is PROLOGUE:
        return 0
    return PROLOGUE.count.get(name, 0) + PAIR.count.get(name, 0) * j


def packed(widths):
    return {n: (sum(w for _, w in widths[:k]), w) for k, (n, w) in enumerate(widths)}


FIRST = packed([("wk0", DIM), ("wk1", DIM), ("wv", 2 * DIM), ("bcol", 5)])
REST = packed([("ident", PART), ("wq0", DIM), ("bv1", DIM), ("iota", EXPERTS), ("wo0", DIM), ("wq1", DIM), ("bo", DIM),
               ("gates", 4), ("rb1", HC), ("rb2", EXPERTS), ("betas", 3),
               ("b1_0", EXPERTS * HC), ("b1_1", EXPERTS * HC)])


def w1_col(l, e):
    return (2 * EXPERTS if e < 0 else l * EXPERTS + e) * HID


def w2_col(l, e, c):
    return 2 * EXPERTS * HC * DIM + c * EXPERTS if e < 0 else ((l * EXPERTS + e) * HC + c) * DIM


def slot_number(plan, j, s):
    return 0 if plan is PROLOGUE else 2 * j + 2 - s


def free_at(base, n, depth):
    return base + max(n - depth, 0)


def flamingo(nc, io, out):
    fp32, fp16, u32 = mybir.dt.float32, mybir.dt.float16, mybir.dt.uint32
    ALU, ACT, AX = mybir.AluOpType, mybir.ActivationFunctionType, mybir.AxisListType
    ctx = ExitStack()
    with ctx:
        def sb(name, shape, dt=fp32):
            return ctx.enter_context(nc.sbuf_tensor(name, shape, dt))

        def sem(name):
            return ctx.enter_context(nc.semaphore(name))

        packs = [(sb(n, [PART, sum(w for _, w in p.values())]), p) for n, p in (("first", FIRST), ("rest", REST))]
        small = {n: t[:, c:c + w] for t, p in packs for n, (c, w) in p.items()}
        ident, iota, wk0, wk1, wv = (small[n] for n in ("ident", "iota", "wk0", "wk1", "wv"))
        wq0, wo0, wq1 = (small[n] for n in ("wq0", "wo0", "wq1"))
        bcol = small["bcol"]
        bv1 = small["bv1"]
        bo, rb1, rb2, gates, betas = (small[n] for n in ("bo", "rb1", "rb2", "gates", "betas"))
        b1 = [small[f"b1_{l}"].rearrange("p (e c) -> p e c", e=EXPERTS) for l in range(2)]
        w1_16 = [sb(f"w1{p}", [DIM, W1_COLS], fp16) for p in ("hi", "lo")]
        wg16 = [w[:, W1_COLS - EXPERTS:W1_COLS] for w in w1_16]
        w2_16 = [sb(f"w2{p}", [PART, W2_COLS], fp16) for p in ("hi", "lo")]
        b2 = [sb(f"b2_{l}", [EXPERTS, DIM]) for l in range(2)]
        tgate = sb("tgate", [PART, 4])
        beta = sb("beta", [PART, 1])
        neghalf = sb("neghalf", [PART, QT])

        xin = [sb(f"xin{s}", [PART, QT, DIM]) for s in range(2)]
        xres = [sb(f"xres{s}", [PART, QT, DIM]) for s in range(2)]
        yT = {0: sb("yT0", [DIM, SEQ]), 1: sb("yT1", [DIM, SEQ]), "q": sb("yTq", [DIM, SEQ])}
        y16 = [[yT[s][:, :].bitcast(fp16)[:, p * SEQ:(p + 1) * SEQ] for p in range(2)] for s in range(2)]
        y = {"q": sb("yq", [PART, QT, DIM]), "x": sb("yx", [PART, QT, DIM])}
        vst = [sb(f"vst{s}", [PART, KT, HEADS, HD + 1]) for s in range(2)]
        k1T = [sb(f"k1T{s}", [DIM, CTX]) for s in range(2)]
        v1 = [sb(f"v1_{s}", [PART, KT, DIM]) for s in range(2)]
        we = [sb(f"we{s}", [PART, QT, EXPERTS]) for s in range(2)]
        we_scaled = [sb(f"we_scaled{s}", [PART, QT, EXPERTS]) for s in range(2)]
        acc = [sb(f"acc{s}", [PART, QT, DIM]) for s in range(2)]
        oproj = acc[1]
        ctxT = sb("ctxT", [DIM, CTX])
        p1T = sb("p1T", [PART, KT, PART])
        halves = p1T[:, :, :].rearrange("p t q -> p (t q)").bitcast(fp16)
        qhi, qlo = sb("qhi", [DIM, SEQ], fp16), sb("qlo", [DIM, SEQ], fp16)
        kst = [sb(f"kst{r}", [PART, CTX], fp16) for r in range(STAGES)]
        k16 = [(kst[2][:, :], kst[3][:, :]), (halves[:, 0:CTX], halves[:, KT * PART:KT * PART + CTX])]
        qst = [sb(f"qst{r}", [PART, GH, SEQ], fp16) for r in range(STAGES)]
        probs = [sb(f"probs{r}", [PART, GH * SEQ]) for r in range(2)]
        hid = [sb(f"hid{r}", [PART, HC, SEQ]) for r in range(2)]
        hid16 = [[p[:, :].bitcast(fp16)[:, h * HID // PART * SEQ:(h + 1) * HID // PART * SEQ]
                  .rearrange("p (c q) -> p c q", c=HC) for h in range(2)] for p in probs]
        probs.append(hid[1][:, :, :].rearrange("p c q -> p (c q)"))
        mxp = sb("mxp", [PART, 2 * GH, len(CHUNKS)])
        mw = sb("mw", [PART, QT, PART])
        m16 = sb("m16", [PART, GH, QT], fp16)
        oTs = sb("oTs", [PART, SEQ])
        rec = sb("rec", [PART, QT, GH])
        attn = sb("attn", [PART, QT, DIM])
        attnT = sb("attnT", [DIM, SEQ])
        q1T = sb("q1T", [DIM, SEQ])
        sc1 = [sb(f"sc1_{k}", [PART, CTX]) for k in range(2 * QT)]
        mx1 = sb("mx1", [PART, 2 * QT, len(CHUNKS)])
        nm1, sum1, rs1 = (sb(n, [PART, 2 * QT]) for n in ("nm1", "sum1", "rs1"))
        bst = sb("bst", [PART, QT, 6])
        mv = sb("mv", [PART, QT, 2])
        vpe, rst, nt1, nt2 = (sb(n, [PART, QT]) for n in ("vpe", "rst", "nt1", "nt2"))
        rr = sb("rr", [PART, QT])
        lg = sb("lg", [PART, QT, EXPERTS])
        eg = sb("eg", [PART, QT, EXPERTS])
        m8 = sb("m8", [PART, QT, 8])
        i8 = sb("i8", [PART, QT, 8], u32)
        i8f = sb("i8f", [PART, QT, 2])
        dm, tm, pr = sb("dm", [PART, QT]), sb("tm", [PART, QT]), sb("pr", [PART, QT, 2])
        nmg, sumg, rg = (sb(n, [PART, QT]) for n in ("nmg", "sumg", "rg"))
        oh = sb("oh", [PART, QT, 2, EXPERTS])
        weT = sb("weT", [EXPERTS, QT, PART])

        pA = [ctx.enter_context(nc.psum_tensor(f"pA{i}", [PART, BANK], fp32)) for i in range(3)]
        pB = [ctx.enter_context(nc.psum_tensor(f"pB{i}", [PART, 2 * BANK], fp32)) for i in range(2)]
        pO = ctx.enter_context(nc.psum_tensor("pO", [PART, BANK], fp32))

        kscr = [nc.dram_tensor(f"kscr{s}", (HEADS, 4, HD, CTX), fp16, kind="Internal").ap() for s in range(2)]
        qscr = [nc.dram_tensor(f"qscr{s}", (HEADS, 4, HD, SEQ), fp16, kind="Internal").ap() for s in range(2)]

        first_in = sem("first_in")
        w_in = sem("w_in")
        we_in = sem("we_in")
        w_split_in = [sem(f"w_split_in{n}") for n in range(len(SPLITS))]
        hi_ready = sem("hi_ready")
        split_dve, split_pool = sem("split_dve"), sem("split_pool")
        hid_hi, hid_lo = sem("hid_hi"), sem("hid_lo")
        pad_in = sem("pad_in")
        zeroed = sem("zeroed")
        x_in = [sem(f"x_in{s}") for s in range(2)]
        ctx_in = sem("ctx_in")
        side_in = [sem(f"side_in{k}") for k in range(2 * QT)]
        stage_in = [sem(f"stage_in{r}") for r in range(STAGES)]
        k_stored = sem("k_stored")
        q_stored = sem("q_stored")
        out_stored = [sem(f"out_stored{s}") for s in range(2)]
        a_full, a_done = sem("a_full"), sem("a_done")
        b_full, b_done = sem("b_full"), sem("b_done")
        pv_full, pv_done = sem("pv_full"), sem("pv_done")
        y_ready = sem("y_ready")
        var_ready, rstd_ready = sem("var_ready"), sem("rstd_ready")
        mw_ready = sem("mw_ready")
        side_scaled = sem("side_scaled")
        coef_ready = sem("coef_ready")
        nm1_ready, p1_ready = sem("nm1_ready"), sem("p1_ready")
        dm_ready, tm_ready = sem("dm_ready"), sem("tm_ready")
        nmg_ready, eg_ready = sem("nmg_ready"), sem("eg_ready")
        we_ready = sem("we_ready")
        x_final = sem("x_final")
        tgate_ready = sem("tgate_ready")
        chain = sem("chain")
        pool_chain = sem("pool_chain")
        passed, pool_passed, sp_passed = sem("passed"), sem("pool_passed"), sem("sp_passed")

        block = ctx.enter_context(nc.Block())

        x_v = io["x"].rearrange("(j s) (q p) d -> j s p q d", s=2, p=PART)
        out_v = out.rearrange("(j s) (q p) d -> j s p q d", s=2, p=PART)
        ctx_v = io["ctxT"].rearrange("(j s) d t -> j s d t", s=2)
        side_v = io["side"].rearrange("(j s) (q p) t -> j s q p t", s=2, p=PART)

        def at(view, it, *rest):
            if isinstance(it, int):
                return view[(it, *rest)]
            return view[bass.ds(it, 1)][(0, *rest)]

        def split_source(n):
            buffer = (sc1 + [hid[0][:, :, :].rearrange("p c q -> p (c q)"), probs[2], probs[0]])[SPLITS[n][3]]
            return buffer[:, 0:SPLITS[n][2]]

        def split_half(n, half):
            k, c, w, _ = SPLITS[n]
            return (w1_16, w2_16)[k][half][:, c:c + w]

        def wait_split(eng, n=len(SPLITS) - 1):
            by_pool = sum(k in BY_POOL for k in range(n + 1))
            if by_pool:
                eng.wait_ge(split_pool, by_pool)
            if n + 1 - by_pool:
                eng.wait_ge(split_dve, n + 1 - by_pool)

        def both(body, eng):
            with eng.Fori(0, PAIRS - 1) as j:
                body(j, PAIR)
            body(PAIRS - 1, LAST)

        @block.sync
        def _(sp):
            def load(dst, src, s):
                sp.dma_start(dst, src).then_inc(s, 16)

            def load_x(j, s):
                load(xin[s][:, :, :], at(x_v, j, s), x_in[s])

            def load_ctx(j, s):
                load(ctxT[:, :], at(ctx_v, j, s), ctx_in)

            def store_k(s, plan, base):
                sp.wait_ge(a_done, base + plan.at["A", ("keys0", s, len(CHUNKS) - 1)])
                sp.sem_inc(sp_passed, 1)
                for p, src in ((1, k16[s][0]), (2, k16[s][1]), (3, k16[s][0])):
                    sp.dma_start(kscr[s][:, p, :, :], src).then_inc(k_stored, 16)

            def store_q(s, plan, base):
                sp.wait_ge(a_done, base + plan.at["A", ("query0", s)])
                sp.sem_inc(sp_passed, 1)
                for p, src in ((1, qhi), (2, qhi), (3, qlo)):
                    sp.dma_start(qscr[s][:, p, :, :], src[:, :]).then_inc(q_stored, 16)

            def stage(i, j):
                s, g, r = i // GROUPS % 2, i % GROUPS, i % STAGES
                if g == 0:
                    sp.wait_ge(k_stored, 48 * (2 * j + i // GROUPS + 1))
                    sp.sem_inc(sp_passed, 1)
                    sp.wait_ge(q_stored, 48 * (2 * j + i // GROUPS + 1))
                    sp.sem_inc(sp_passed, 1)
                if i >= STAGES:
                    sp.wait_ge(b_full, before("B", j) + PAIR.at["B", ("s2", i - STAGES, KT - 1)])
                    sp.sem_inc(sp_passed, 1)
                sp.dma_start(kst[r][:, :], kscr[s][g * GH:(g + 1) * GH].rearrange("h p c t -> (h p c) t"))\
                    .then_inc(stage_in[r], 16)
                for h in range(GH):
                    sp.dma_start(qst[r][ROWS * h:ROWS * (h + 1), h, :],
                                 qscr[s][g * GH + h].rearrange("p c q -> (p c) q")).then_inc(stage_in[r], 16)

            def load_weights(n):
                k, c, w, _ = SPLITS[n]
                if n >= len(BUFFER_COLS):
                    wait_split(sp, n - len(BUFFER_COLS))
                load(split_source(n), io[f"w_split{k}"][:, c:c + w], w_split_in[n])

            def load_pads(s):
                sp.dma_start(kscr[s][:, 0, :, :], io["kpad"]).then_inc(pad_in, 16)
                sp.dma_start(qscr[s][:, 0, :, :], io["qpad"]).then_inc(pad_in, 16)

            load(packs[0][0][:, :], io["first"], first_in)
            load_ctx(0, 0)
            load_x(0, 0)
            for n in range(WEIGHTS_FIRST):
                load_weights(n)
            load(packs[1][0][:, :], io["rest"], w_in)
            load_pads(0)
            store_k(0, PROLOGUE, 0)
            store_q(0, PROLOGUE, 0)
            sp.wait_ge(pad_in, 32)
            sp.wait_ge(zeroed, 2)
            stage(0, 0)
            stage(1, 0)
            sp.wait_ge(b_full, PROLOGUE.at["B", ("values", 0, LAST_VALUES)])
            for n in range(WEIGHTS_FIRST, len(BUFFER_COLS)):
                load_weights(n)
            load_ctx(0, 1)
            load_x(0, 1)
            stage(2, 0)
            stage(3, 0)
            load_pads(1)
            for s in range(2):
                sp.sem_inc(out_stored[s], 16)
            for l in range(2):
                load(b2[l][:, :], io[f"b2_{l}"], we_in)
            for n in range(len(BUFFER_COLS), len(SPLITS)):
                load_weights(n)
            sp.wait_ge(pad_in, 64)

            def body(j, plan):
                more = plan is PAIR
                base = before("A", j)
                sp.wait_ge(a_full, base)
                sp.sem_inc(sp_passed, 1)
                wait_split(sp)
                for k in range(2 * QT):
                    load(sc1[k][:, :], at(side_v, j, k // QT, k % QT), side_in[k])
                store_k(1, plan, base)
                store_q(1, plan, base)
                if more:
                    sp.wait_ge(b_full, before("B", j) + plan.at["B", ("values", 1, LAST_VALUES)])
                    sp.sem_inc(sp_passed, 1)
                    load_ctx(j + 1, 0)
                for i in range(STAGES, NG):
                    stage(i, j)
                if more:
                    for s in range(2):
                        sp.wait_ge(y_ready, before("finish", j) + plan.at["finish", ("finish", s, "m0")])
                        sp.sem_inc(sp_passed, 1)
                        load_x(j + 1, s)
                    store_k(0, plan, base)
                    sp.wait_ge(b_full, before("B", j) + plan.at["B", ("values", 0, LAST_VALUES)])
                    sp.sem_inc(sp_passed, 1)
                    load_ctx(j + 1, 1)
                    store_q(0, plan, base)
                    for i in range(NG, NG + STAGES):
                        stage(i, j)
                for s in range(2):
                    sp.wait_ge(x_final, 2 * j + s + 1)
                    sp.sem_inc(sp_passed, 1)
                    sp.dma_start(at(out_v, j, s), xres[s][:, :, :]).then_inc(out_stored[s], 16)

            both(body, sp)
            for s in range(2):
                sp.wait_ge(out_stored[s], 16 * (PAIRS + 1))

        @block.gpsimd
        def _(pool):
            pool.memset(neghalf[:, :], -0.5).then_inc(zeroed, 1)
            pool.wait_ge(zeroed, 1)

            def run(plan, j):
                for kind, *a in plan.steps:
                    if kind == "norm":
                        pool.wait_ge(var_ready, before("norm", j, plan) + plan.at["norm", (kind, *a)])
                        pool.tensor_tensor(rst[:, :], vpe[:, :], neghalf[:, :], ALU.pow).then_inc(rstd_ready, 1)
                    elif kind == "split" and a[0] in BY_POOL:
                        n, = a
                        src = split_source(n)
                        pool.wait_ge(hi_ready, n + 1)
                        pool.tensor_scalar(src, src, W_SCALE, None, ALU.mult).then_inc(pool_chain, 1)
                        pool.wait_ge(pool_chain, BY_POOL.index(n) + 1)
                        pool.tensor_tensor(split_half(n, 1), src, split_half(n, 0), ALU.subtract).then_inc(split_pool, 1)
                    elif kind == "halve" and not halved_by_vector(*a):
                        r = hid_ring(*a)
                        pool.wait_ge(hid_hi, before("halve", j) + plan.at["halve", (kind, *a)])
                        pool.tensor_tensor(hid16[r][1], hid[r][:, :, :], hid16[r][0], ALU.subtract).then_inc(hid_lo, 1)
                    elif kind == "scale_side":
                        k, = a
                        pool.wait_ge(side_in[k], 16 * (j + 1))
                        pool.sem_inc(pool_passed, 1)
                        pool.tensor_scalar(sc1[k][:, :], sc1[k][:, :], beta[:, 0:1], 0.0, ALU.mult, ALU.add)\
                            .then_inc(side_scaled, 1)

            run(PROLOGUE, 0)
            pool.wait_ge(coef_ready, 1)
            both(lambda j, plan: run(plan, j), pool)

        @block.scalar
        def _(act):
            act.wait_ge(first_in, 16)

            def upper_halves(n):
                act.wait_ge(w_split_in[n], 16)
                act.activation(split_half(n, 0), split_source(n), ACT.Identity, scale=W_SCALE).then_inc(hi_ready, 1)

            def run(plan, j):
                def next_b(step):
                    n = plan.unit("B", step)
                    act.wait_ge(b_full, before("B", j, plan) + n)
                    return pB[(n - 1) % 2]

                for step in plan.steps:
                    kind, *a = step
                    if kind == "keys1":
                        s, h = a
                        c0 = 2 * BANK * h
                        w = min(2 * BANK, CTX - c0)
                        banks = next_b((kind, *a))
                        act.activation(k1T[s][:, c0:c0 + w], banks[:, 0:w], ACT.Identity, bias=bcol[:, 3:4])\
                            .then_inc(b_done, 1)
                    elif kind == "values":
                        s, t0 = a
                        banks = next_b((kind, *a))
                        m = min(4, KT - t0)
                        kr = tile_rows(t0 + m - 1)
                        src = banks[0:kr, 0:m * 2 * DIM].rearrange("p (t v) -> p t v", t=m)
                        act.activation(v1[s][0:kr, t0:t0 + m, :], src[:, :, DIM:2 * DIM], ACT.Identity)
                        act.activation(vst[s][0:kr, t0:t0 + m, :, 0:HD],
                                       src[:, :, 0:DIM].rearrange("p t (h c) -> p t h c", c=HD), ACT.Identity)\
                            .then_inc(b_done, 1)
                    elif kind == "s2":
                        i, t = a
                        n, kr = i * KT + t, tile_rows(t)
                        banks = next_b((kind, *a))
                        act.activation(probs[n % 3][0:kr, :], banks[0:kr, :], ACT.Exp, scale=HD ** -0.5)\
                            .then_inc(b_done, 1)
                    elif kind == "up":
                        l, s, e, c = a
                        if c < HC - 1:
                            continue
                        if e == hidden(l, 0)[0][2] and l == s == 0:
                            act.wait_ge(we_in, 16 * 2)
                        r = hid_ring(l, s, e)
                        banks = next_b((kind, *a))
                        n = before("up", j) + plan.at["up", step]
                        act.wait_ge(hid_lo, n)
                        for c in range(HC):
                            last = act.activation(hid[r][:, c, :], banks[:, c * SEQ:(c + 1) * SEQ],
                                                  ACT.Silu if l == 0 else ACT.Gelu, scale=UNSCALE,
                                                  bias=rb1[:, c:c + 1] if e < 0 else b1[l][:, e, c:c + 1])
                        last.then_inc(b_done, 1)
                        act.wait_ge(b_done, before("B", j) + plan.unit("B", step))
                        if (l, s) == (0, 0):
                            act.wait_ge(pv_full, NG * (j + 1))
                        if l == 1 and s == 0 and e < 2:
                            act.wait_ge(a_full, before("A", j) + plan.at["A", ("down",) + (hidden(0, 1)[-1])])
                        elif (l, s, e) not in hidden(0, 0)[:2]:
                            ups = hidden(l, 0) + hidden(l, 1)
                            act.wait_ge(a_full, before("A", j) + plan.at["A", ("down",) + ups[ups.index((l, s, e)) - 2]])
                        act.activation(hid16[r][0], hid[r][:, :, :], ACT.Identity,
                                       scale=HID_SCALE[l]).then_inc(hid_hi, 1)
                    elif kind == "tanh":
                        act.wait_ge(dm_ready, 2 * j + a[0] + 1)
                        act.activation(tm[:, :], dm[:, :], ACT.Tanh, scale=0.5).then_inc(tm_ready, 1)
                    elif kind == "exp1":
                        k, = a
                        act.wait_ge(nm1_ready, 2 * QT * j + k + 1)
                        act.activation(sc1[k][:, :], sc1[k][:, :], ACT.Exp, bias=nm1[:, k:k + 1],
                                       accum_out=sum1[:, k:k + 1]).then_inc(p1_ready, 1)
                    elif kind == "split":
                        upper_halves(a[0])
                    elif kind == "exp_gate":
                        act.wait_ge(nmg_ready, 2 * j + a[0] + 1)
                        for r in range(QT):
                            last = act.activation(eg[:, r, :], lg[:, r, :], ACT.Exp, bias=nmg[:, r:r + 1],
                                                  accum_out=sumg[:, r:r + 1])
                        last.then_inc(eg_ready, 1)

            run(PROLOGUE, 0)
            act.wait_ge(w_in, 16)
            act.activation(tgate[:, :], gates[:, :], ACT.Tanh).then_inc(tgate_ready, 1)
            wait_split(act)
            both(lambda j, plan: run(plan, j), act)

        @block.tensor
        def _(pe):
            mm, turn = nc.tensor.matmul, nc.tensor.transpose

            def run(plan, j):
                base_a, base_b = before("A", j, plan), before("B", j, plan)

                def open_a():
                    n = plan.unit("A", step)
                    pe.wait_ge(a_done, free_at(base_a, n, 3))
                    return pA[(n - 1) % 3]

                def open_b():
                    n = plan.unit("B", step)
                    pe.wait_ge(b_done, free_at(base_b, n, 2))
                    return pB[(n - 1) % 2]

                def turn_two(bank, src, rows=PART):
                    for r in range(QT):
                        last = turn(bank[0:rows, r * PART:(r + 1) * PART], src(r), ident[:, :])
                    last.then_inc(a_full, 1)

                for step in plan.steps:
                    kind, *a = step
                    if kind == "keys0":
                        s, c = a
                        c0, w = CHUNKS[c]
                        bank = open_a()
                        if c == 0:
                            pe.wait_ge(ctx_in, 16 * (slot_number(plan, j, s) + 1))
                        mm(bank[:, 0:w], wk0[:, :], ctxT[:, c0:c0 + w], start=True, stop=True).then_inc(a_full, 1)
                    elif kind == "keys1":
                        s, h = a
                        c0 = 2 * BANK * h
                        banks = open_b()
                        for o in range(0, min(2 * BANK, CTX - c0), BANK):
                            m = min(BANK, CTX - c0 - o)
                            last = mm(banks[:, o:o + m], wk1[:, :], ctxT[:, c0 + o:c0 + o + m], start=True, stop=True)
                        last.then_inc(b_full, 1)
                    elif kind == "values":
                        s, t0 = a
                        banks = open_b()
                        for t in range(t0, min(t0 + 4, KT)):
                            kr = tile_rows(t)
                            last = mm(banks[0:kr, (t - t0) * 2 * DIM:(t - t0 + 1) * 2 * DIM],
                                      ctxT[:, t * PART:t * PART + kr], wv[:, :], start=True, stop=True)
                        last.then_inc(b_full, 1)
                    elif kind == "turn":
                        s, what = a
                        bank = open_a()
                        if plan is PROLOGUE:
                            pe.wait_ge(w_in, 16)
                        pe.wait_ge(y_ready, before("finish", j, plan) + plan.at["finish", ("finish", s, what)])
                        turn_two(bank, lambda r: y["q" if what == "q" else "x"][:, r, :])
                    elif kind in ("query0", "query1"):
                        s, = a
                        bank = open_a()
                        pe.wait_ge(a_done, base_a + plan.at["A", ("turn", s, "q" if kind == "query0" else "a1")])
                        w, src = (wq0, yT["q"]) if kind == "query0" else (wq1, yT[s])
                        mm(bank[:, 0:SEQ], w[:, :], src[:, :], start=True, stop=True).then_inc(a_full, 1)
                    elif kind == "s1":
                        i, u, c = a
                        c0, w = CHUNKS[c]
                        h, r, st = u // QT, u % QT, i % STAGES
                        bank = open_a()
                        if u == 0 and c == 0:
                            pe.wait_ge(stage_in[st], 16 * (1 + GH) * (2 * j + i // STAGES + 1))
                        mm(bank[:, 0:w], qst[st][:, h, r * PART:(r + 1) * PART], kst[st][:, c0:c0 + w],
                           start=True, stop=True).then_inc(a_full, 1)
                    elif kind == "s1_rest":
                        i, half = a
                        c0, w = CHUNKS[-1]
                        st = i % STAGES
                        bank = open_a()
                        for n in range(GH):
                            h, r = divmod(GH * half + n, QT)
                            last = mm(bank[:, n * w:(n + 1) * w], qst[st][:, h, r * PART:(r + 1) * PART],
                                      kst[st][:, c0:c0 + w], start=True, stop=True)
                        last.then_inc(a_full, 1)
                    elif kind == "put_max":
                        bank = open_a()
                        pe.wait_ge(mw_ready, before("split_max", j, plan) + plan.at["split_max", ("split_max", a[0])])
                        turn_two(bank, lambda r: mw[:, r, :])
                    elif kind == "s2":
                        i, t = a
                        kr, st = tile_rows(t), i % STAGES
                        banks = open_b()
                        if t == 0:
                            pe.wait_ge(a_done, base_a + (plan.at["A", ("put_max", i)] if i >= PRE else 0))
                        for h in range(0, GH, 2):
                            last = mm(banks[0:kr, h * SEQ:(h + 2) * SEQ], kst[st][:, t * PART:t * PART + kr],
                                      qst[st][:, h:h + 2, :], start=True, stop=True)
                        last.then_inc(b_full, 1)
                    elif kind == "weigh":
                        i, t = a
                        n, kr, s = i * KT + t, tile_rows(t), i // GROUPS
                        if t == 0:
                            pe.wait_ge(pv_done, NG * j + i + 1)
                        pe.wait_ge(b_done, base_b + plan.at["B", ("s2", i, t)])
                        for h in range(GH):
                            last = mm(pO[ROWS * h:ROWS * h + HD + 1, 0:SEQ], vst[s][0:kr, t, (i % GROUPS) * GH + h, :],
                                      probs[n % 3][0:kr, h * SEQ:(h + 1) * SEQ], start=(t == 0), stop=(t == KT - 1))
                        if t == KT - 1:
                            last.then_inc(pv_full, 1)
                    elif kind == "turn_out":
                        bank = open_a()
                        pe.wait_ge(pv_done, NG * j + a[0] + 2)
                        turn_two(bank, lambda r: oTs[:, r * PART:(r + 1) * PART])
                    elif kind == "turn_attn":
                        s, = a
                        bank = open_a()
                        pe.wait_ge(a_done, base_a + plan.at["A", ("turn_out", GROUPS * (s + 1) - 1)])
                        turn_two(bank, lambda r: attn[:, r, :])
                    elif kind == "project":
                        bank = open_a()
                        pe.wait_ge(a_done, base_a + plan.at["A", ("turn_attn", a[0])])
                        for r in range(QT):
                            last = mm(bank[:, r * DIM:(r + 1) * DIM], attnT[:, r * PART:(r + 1) * PART], wo0[:, :],
                                      start=True, stop=True)
                        last.then_inc(a_full, 1)
                    elif kind == "up":
                        l, s, e, c = a
                        if c == 0:
                            banks_up = open_b()
                            if (l, s, e) == hidden(l, s)[0]:
                                pe.wait_ge(a_done, base_a + plan.at["A", ("turn", s, f"m{l}")])
                                if l == s == 0:
                                    wait_split(pe)
                        for n, (wh, yh) in enumerate(HALVES):
                            c0 = w1_col(l, e) + c * PART
                            last = mm(banks_up[:, c * SEQ:(c + 1) * SEQ], w1_16[wh][:, c0:c0 + PART], y16[s][yh], start=(n == 0), stop=(n == 2))
                        if c == HC - 1:
                            last.then_inc(b_full, 1)
                    elif kind == "down":
                        l, s, e = a
                        h16 = hid16[hid_ring(l, s, e)]
                        bank = open_a()
                        pe.wait_ge(hid_lo, before("halve", j) + plan.at["halve", ("halve", l, s, e)] + 2)
                        n = EXPERTS if e < 0 else DIM
                        terms = [(c, hh, wh) for c in range(HC) for hh, wh in HALVES]
                        for r in range(QT):
                            for c, hh, wh in terms:
                                c0 = w2_col(l, e, c)
                                last = mm(bank[:, r * n:(r + 1) * n], h16[hh][:, c, r * PART:(r + 1) * PART],
                                          w2_16[wh][:, c0:c0 + n], start=((c, hh, wh) == terms[0]),
                                          stop=((c, hh, wh) == terms[-1]))
                        last.then_inc(a_full, 1)
                    elif kind == "gate":
                        s, = a
                        bank = open_a()
                        pe.wait_ge(a_done, base_a + plan.at["A", ("turn", s, "m1")])
                        for r in range(QT):
                            for n, (wh, yh) in enumerate(HALVES):
                                last = mm(bank[:, r * EXPERTS:(r + 1) * EXPERTS], y16[s][yh][:, r * PART:(r + 1) * PART],
                                          wg16[wh][:, :], start=(n == 0), stop=(n == 2))
                        last.then_inc(a_full, 1)
                    elif kind == "turn_we":
                        l, s = a
                        bank = open_a()
                        pe.wait_ge(we_ready, 4 * j + 2 * l + s + 1)
                        turn_two(bank, lambda r: we[s][:, r, :], EXPERTS)
                    elif kind == "bias2":
                        l, s = a
                        bank = open_a()
                        pe.wait_ge(a_done, base_a + plan.at["A", ("turn_we", l, s)])
                        for r in range(QT):
                            last = mm(bank[:, r * DIM:(r + 1) * DIM], weT[:, r, :], b2[l][:, :], start=True, stop=True)
                        last.then_inc(a_full, 1)
                    elif kind == "qk":
                        k, c = a
                        c0, w = CHUNKS[c]
                        bank = open_a()
                        if c == 0:
                            pe.wait_ge(a_done, base_a + plan.at["A", ("query1", k // QT)])
                        mm(bank[:, 0:w], q1T[:, k % QT * PART:(k % QT + 1) * PART], k1T[k // QT][:, c0:c0 + w],
                           start=True, stop=True).then_inc(a_full, 1)
                    elif kind == "turn_p":
                        k, b = a
                        if b == 0:
                            pe.wait_ge(p1_ready, 2 * QT * j + k + 1)
                        bank = open_a()
                        for t in range(4 * b, min(4 * b + 4, KT)):
                            kr = tile_rows(t)
                            last = turn(bank[0:kr, t % 4 * PART:(t % 4 + 1) * PART], sc1[k][:, t * PART:t * PART + kr],
                                        ident[:, :])
                        last.then_inc(a_full, 1)
                    elif kind == "out1":
                        k, = a
                        bank = open_a()
                        pe.wait_ge(a_done, base_a + plan.at["A", ("turn_p", k, (KT - 1) // 4)])
                        for t in range(KT):
                            kr = tile_rows(t)
                            last = mm(bank[:, 0:DIM], p1T[0:kr, t, :], v1[k // QT][0:kr, t, :],
                                      start=(t == 0), stop=(t == KT - 1))
                        last.then_inc(a_full, 1)

            pe.wait_ge(first_in, 16)
            run(PROLOGUE, 0)
            both(lambda j, plan: run(plan, j), pe)

        @block.vector
        def _(dve):
            v = nc.vector

            def run(plan, j):
                base_a = before("A", j, plan)
                links = [0 if plan is PROLOGUE else 2 + before("links", j), 0]
                taken = [0]
                mw_of = mw[:, :, :].rearrange("p q (h r) -> p h q r", h=GH)

                def link(ins, alone=False):
                    links[1] += 1
                    ins.then_inc(chain, 1)
                    dve.wait_ge(chain, links[0] + links[1])
                    if alone:
                        dve.sem_inc(passed, 1)

                def next_a(alone=False):
                    taken[0] = n = plan.unit("A", step)
                    dve.wait_ge(a_full, base_a + n)
                    if alone:
                        dve.sem_inc(passed, 1)
                    return pA[(n - 1) % 3]

                def done():
                    return base_a + taken[0]

                def top_two(l, s):
                    for r in range(QT):
                        last = v.max(m8[:, r, :], lg[:, r, :])
                    link(last)
                    if l == 0:
                        v.tensor_tensor(dm[:, :], m8[:, :, 0], m8[:, :, 1], ALU.subtract).then_inc(dm_ready, 1)
                    else:
                        v.tensor_scalar(nmg[:, :], m8[:, :, 0], -1.0, None, ALU.mult).then_inc(nmg_ready, 1)
                    for r in range(QT):
                        last = v.max_index(i8[:, r, :], m8[:, r, :], lg[:, r, :])
                    link(last)
                    link(v.tensor_copy(i8f[:, :, :], i8[:, :, 0:2]))

                def weights_of_two(l, s):
                    if l == 0:
                        dve.wait_ge(tm_ready, 2 * j + s + 1)
                        v.tensor_scalar(pr[:, :, 0], tm[:, :], 0.5, 0.5, ALU.mult, ALU.add)
                        link(v.tensor_scalar(pr[:, :, 1], tm[:, :], -0.5, 0.5, ALU.mult, ALU.add))
                    else:
                        dve.wait_ge(eg_ready, 2 * j + s + 1)
                        link(v.reciprocal(rg[:, :], sumg[:, :]))
                    for r in range(QT):
                        for k in range(2):
                            w = pr[:, r, k:k + 1] if l == 0 else rg[:, r:r + 1]
                            last = v.tensor_scalar(oh[:, r, k, :], iota[:, :], i8f[:, r, k:k + 1], w,
                                                   ALU.is_equal, ALU.mult)
                    link(last)
                    if l == 0:
                        v.tensor_tensor(we[s][:, :, :], oh[:, :, 0, :], oh[:, :, 1, :], ALU.add).then_inc(we_ready, 1)
                    else:
                        link(v.tensor_tensor(oh[:, :, 0, :], oh[:, :, 0, :], oh[:, :, 1, :], ALU.add))
                        v.tensor_tensor(we[s][:, :, :], oh[:, :, 0, :], eg[:, :, :], ALU.mult).then_inc(we_ready, 1)
                    dve.wait_ge(we_ready, 4 * j + 2 * l + s + 1)
                    link(v.tensor_scalar(we_scaled[s][:, :, :], we[s][:, :, :], 1 / (W_SCALE * HID_SCALE[l]), None, ALU.mult))

                for step in plan.steps:
                    kind, *a = step
                    if kind == "keys0":
                        s, c = a
                        c0, w = CHUNKS[c]
                        bank = next_a()
                        if c == 0 and plan is not PROLOGUE:
                            dve.wait_ge(k_stored, 48 * slot_number(plan, j, s))
                        khi, klo = k16[s]
                        link(v.tensor_scalar(khi[:, c0:c0 + w], bank[:, 0:w], bcol[:, 1:2], None, ALU.add))
                        v.scalar_tensor_tensor(klo[:, c0:c0 + w], bank[:, 0:w], bcol[:, 1:2], khi[:, c0:c0 + w],
                                               op0=ALU.add, op1=ALU.subtract).then_inc(a_done, 1)
                    elif kind == "norm":
                        s, what = a
                        src = xin[s] if what == "q" else xres[s]
                        if what == "q":
                            dve.wait_ge(x_in[s], 16 if plan is PROLOGUE else 16 * (j + 2 - s))
                        for r in range(QT):
                            last = v.bn_stats(bst[:, r, :], src[:, r, :])
                        link(last, alone=True)
                        for r in range(QT):
                            last = v.bn_aggr(mv[:, r, :], bst[:, r, :])
                        link(last)
                        v.tensor_scalar(vpe[:, :], mv[:, :, 1], EPS, None, ALU.add).then_inc(var_ready, 1)
                    elif kind == "finish":
                        s, what = a
                        src = xin[s] if what == "q" else xres[s]
                        dst = y["q" if what == "q" else "x"]
                        dve.wait_ge(rstd_ready, before("finish", j, plan) + plan.at["finish", step])
                        link(v.tensor_tensor(nt1[:, :], rst[:, :], rst[:, :], ALU.mult))
                        link(v.tensor_tensor(nt2[:, :], nt1[:, :], vpe[:, :], ALU.mult))
                        link(v.tensor_scalar(nt1[:, :], nt2[:, :], -0.5, 1.5, ALU.mult, ALU.add))
                        link(v.tensor_tensor(rr[:, :], nt1[:, :], rst[:, :], ALU.mult))
                        for r in range(QT):
                            last = v.tensor_scalar(dst[:, r, :], src[:, r, :], mv[:, r, 0:1], rr[:, r:r + 1],
                                                   ALU.subtract, ALU.mult)
                        last.then_inc(y_ready, 1)
                    elif kind == "turn":
                        s, what = a
                        bank = next_a()
                        if what in ("m0", "m1"):
                            link(v.tensor_scalar(y16[s][0], bank[:, 0:SEQ], Y_SCALE, None, ALU.mult))
                            v.scalar_tensor_tensor(y16[s][1], bank[:, 0:SEQ], Y_SCALE, y16[s][0],
                                                   op0=ALU.mult, op1=ALU.subtract).then_inc(a_done, 1)
                        else:
                            v.tensor_copy(yT["q" if what == "q" else s][:, :], bank[:, 0:SEQ]).then_inc(a_done, 1)
                    elif kind == "query0":
                        s, = a
                        bank = next_a()
                        if plan is not PROLOGUE:
                            dve.wait_ge(q_stored, 48 * slot_number(plan, j, s))
                        link(v.tensor_scalar(qhi[:, :], bank[:, 0:SEQ], bcol[:, 0:1], None, ALU.add))
                        v.scalar_tensor_tensor(qlo[:, :], bank[:, 0:SEQ], bcol[:, 0:1], qhi[:, :],
                                               op0=ALU.add, op1=ALU.subtract).then_inc(a_done, 1)
                    elif kind == "s1":
                        i, u, c = a
                        bank = next_a()
                        v.reduce_max(mxp[:, u, c:c + 1], bank[:, 0:CHUNKS[c][1]], axis=AX.X).then_inc(a_done, 1)
                    elif kind == "s1_rest":
                        i, half = a
                        w = CHUNKS[-1][1]
                        bank = next_a()
                        v.reduce_max(mxp[:, GH * half:GH * (half + 1), len(CHUNKS) - 1],
                                     bank[:, 0:GH * w].rearrange("p (n t) -> p n t", n=GH), axis=AX.X).then_inc(a_done, 1)
                    elif kind == "split_max":
                        dve.wait_ge(a_done, done())
                        link(v.tensor_reduce(mw_of[:, :, :, 0], mxp[:, :, :].rearrange("p (h q) c -> p h q c", h=GH),
                                             axis=AX.X, op=ALU.max, negate=True))
                        link(v.tensor_scalar(m16[:, :, :], mw_of[:, :, :, 0], 1 / MAX_SCALE, None, ALU.mult))
                        v.scalar_tensor_tensor(mw_of[:, :, :, 1], m16[:, :, :], -MAX_SCALE, mw_of[:, :, :, 0],
                                               op0=ALU.mult, op1=ALU.add).then_inc(mw_ready, 1)
                    elif kind == "put_max":
                        i, = a
                        bank = next_a()
                        for h in range(GH):
                            p = ROWS * h
                            last = v.tensor_scalar(qst[i % STAGES][p:p + 2, h, :], bank[p:p + 2, 0:SEQ],
                                                   1 / MAX_SCALE, None, ALU.mult)
                        last.then_inc(a_done, 1)
                    elif kind == "keep_out":
                        dve.wait_ge(pv_full, NG * j + a[0] + 1)
                        v.tensor_copy(oTs[:, :], pO[:, 0:SEQ]).then_inc(pv_done, 1)
                    elif kind == "turn_out":
                        g = a[0] % GROUPS
                        bank = next_a()
                        o = bank[:, 0:SEQ].rearrange("p (q h r) -> p q h r", q=QT, h=GH)
                        link(v.reciprocal(rec[:, :, :], o[:, :, :, HD]))
                        dst = attn[:, :, g * GH * HD:(g + 1) * GH * HD].rearrange("p q (h c) -> p q h c", c=HD)
                        v.tensor_tensor(dst, o[:, :, :, 0:HD], rec[:, :, :].unsqueeze(3).broadcast_to([PART, QT, GH, HD]),
                                        ALU.mult).then_inc(a_done, 1)
                    elif kind == "turn_attn":
                        bank = next_a()
                        v.tensor_scalar(attnT[:, :], bank[:, 0:SEQ], bcol[:, 4:5], None, ALU.add).then_inc(a_done, 1)
                    elif kind == "project":
                        s, = a
                        bank = next_a()
                        for r in range(QT):
                            last = v.tensor_tensor(oproj[:, r, :], bank[:, r * DIM:(r + 1) * DIM], bo[:, :], ALU.add)
                        last.then_inc(a_done, 1)
                        dve.wait_ge(a_done, done())
                        dve.wait_ge(out_stored[s], 16 * (j + 1))
                        link(v.scalar_tensor_tensor(xres[s][:, :, :], oproj[:, :, :], tgate[:, 0:1], xin[s][:, :, :],
                                                    op0=ALU.mult, op1=ALU.add))
                    elif kind in ("down", "gate") and (kind == "gate" or a[2] < 0):
                        l, s = (1, a[0]) if kind == "gate" else (0, a[1])
                        bank = next_a()
                        for r in range(QT):
                            src = bank[:, r * EXPERTS:(r + 1) * EXPERTS]
                            last = (v.scalar_tensor_tensor(lg[:, r, :], src, 1 / (W_SCALE * HID_SCALE[0]), rb2[:, :],
                                                           op0=ALU.mult, op1=ALU.add) if l == 0
                                    else v.tensor_scalar(lg[:, r, :], src, UNSCALE, None, ALU.mult))
                        last.then_inc(a_done, 1)
                        dve.wait_ge(a_done, done())
                        dve.sem_inc(passed, 1)
                        top_two(l, s)
                    elif kind == "halve" and halved_by_vector(*a):
                        r = hid_ring(*a)
                        if a[0] == 1:
                            dve.wait_ge(hid_lo, before("halve", j) + plan.at["halve", step] + 1)
                        dve.wait_ge(hid_hi, before("halve", j) + plan.at["halve", step])
                        v.scalar_tensor_tensor(hid16[r][1], hid[r][:, :, :], HID_SCALE[a[0]], hid16[r][0],
                                               op0=ALU.mult, op1=ALU.subtract).then_inc(hid_lo, 1)
                    elif kind == "split" and a[0] not in BY_POOL:
                        n, = a
                        dve.wait_ge(hi_ready, n + 1)
                        v.scalar_tensor_tensor(split_half(n, 1), split_source(n), W_SCALE, split_half(n, 0),
                                               op0=ALU.mult, op1=ALU.subtract).then_inc(split_dve, 1)
                    elif kind == "pick":
                        weights_of_two(*a)
                    elif kind == "down":
                        l, s, e = a
                        bank = next_a()
                        if e:
                            dve.wait_ge(a_done, base_a + plan.at["A", ("down", l, s, e - 1)])
                        for r in range(QT):
                            src = bank[:, r * DIM:(r + 1) * DIM]
                            if e == 0:
                                last = v.tensor_scalar(acc[s][:, r, :], src, we_scaled[s][:, r, e:e + 1], None, ALU.mult)
                            else:
                                last = v.scalar_tensor_tensor(acc[s][:, r, :], src, we_scaled[s][:, r, e:e + 1],
                                                              acc[s][:, r, :], op0=ALU.mult, op1=ALU.add)
                        last.then_inc(a_done, 1)
                    elif kind == "turn_we":
                        bank = next_a()
                        v.tensor_copy(weT[:, :, :], bank[0:EXPERTS, 0:SEQ].rearrange("e (q p) -> e q p", q=QT))\
                            .then_inc(a_done, 1)
                    elif kind == "bias2":
                        l, s = a
                        bank = next_a()
                        dve.wait_ge(a_done, base_a + plan.at["A", ("down", l, s, EXPERTS - 1)])
                        v.tensor_tensor(acc[s][:, :, :], bank[:, 0:QT * DIM].rearrange("p (q d) -> p q d", q=QT),
                                        acc[s][:, :, :], ALU.add).then_inc(a_done, 1)
                        dve.wait_ge(a_done, done())
                        ins = v.scalar_tensor_tensor(xres[s][:, :, :], acc[s][:, :, :], tgate[:, 2 + l:3 + l],
                                                     xres[s][:, :, :], op0=ALU.mult, op1=ALU.add)
                        if l == 0:
                            link(ins)
                        else:
                            ins.then_inc(x_final, 1)
                    elif kind == "query1":
                        s, = a
                        link(v.tensor_tensor(xres[s][:, :, :], xres[s][:, :, :],
                                             bv1[:, :].unsqueeze(1).broadcast_to([PART, QT, DIM]), ALU.add))
                        bank = next_a()
                        v.tensor_scalar(q1T[:, :], bank[:, 0:SEQ], bcol[:, 2:3], DIM ** -0.5, ALU.add, ALU.mult)\
                            .then_inc(a_done, 1)
                    elif kind == "qk":
                        k, c = a
                        c0, w = CHUNKS[c]
                        if c == 0:
                            dve.wait_ge(side_scaled, 2 * QT * j + k + 1)
                            dve.sem_inc(passed, 1)
                        bank = next_a(alone=True)
                        v.tensor_tensor_reduce(out=sc1[k][:, c0:c0 + w], in0=bank[:, 0:w], in1=sc1[k][:, c0:c0 + w],
                                               scale=1.0, scalar=-3.0e38, op0=ALU.add, op1=ALU.max,
                                               accum_out=mx1[:, k, c:c + 1]).then_inc(a_done, 1)
                    elif kind == "max1":
                        k, = a
                        dve.wait_ge(a_done, done())
                        v.tensor_reduce(nm1[:, k:k + 1], mx1[:, k, :], axis=AX.X, op=ALU.max, negate=True)\
                            .then_inc(nm1_ready, 1)
                    elif kind == "turn_p":
                        k, b = a
                        t0 = 4 * b
                        m = min(4, KT - t0)
                        kr = tile_rows(t0 + m - 1)
                        bank = next_a()
                        if k == 0 and b == 0:
                            dve.wait_ge(k_stored, 48 * (2 * j + 2))
                        v.tensor_copy(p1T[0:kr, t0:t0 + m, :],
                                      bank[0:kr, 0:m * PART].rearrange("p (t q) -> p t q", t=m)).then_inc(a_done, 1)
                    elif kind == "out1":
                        k, = a
                        s, r = k // QT, k % QT
                        dve.wait_ge(p1_ready, 2 * QT * j + k + 1)
                        link(v.reciprocal(rs1[:, k:k + 1], sum1[:, k:k + 1]))
                        link(v.tensor_tensor(rs1[:, k:k + 1], rs1[:, k:k + 1], tgate[:, 1:2], ALU.mult))
                        bank = next_a()
                        v.scalar_tensor_tensor(xres[s][:, r, :], bank[:, 0:DIM], rs1[:, k:k + 1], xres[s][:, r, :],
                                               op0=ALU.mult, op1=ALU.add).then_inc(a_done, 1)
                        if r == QT - 1:
                            dve.wait_ge(a_done, done())
                assert links[1] == plan.count["links"], (links, plan.count["links"])

            v.memset(mw[:, :, :], 0.0)
            for r in range(STAGES):
                v.memset(qst[r][:, :, :].bitcast(fp32), 0.0)
            for s in range(2):
                v.memset(vst[s][:, :, :, :], 1.0)
            dve.sem_inc(hid_lo, 2)
            v.memset(pO[:, :], 0.0).then_inc(pv_done, 1)
            dve.wait_ge(pv_done, 1)
            v.memset(rec[:, :, :], 0.0).then_inc(zeroed, 1)
            dve.wait_ge(first_in, 16)
            dve.wait_ge(zeroed, 2)
            run(PROLOGUE, 0)
            dve.wait_ge(w_in, 16)
            v.tensor_tensor(beta[:, :], betas[:, 0:1], betas[:, 1:2], ALU.add).then_inc(chain, 1)
            dve.wait_ge(chain, PROLOGUE.count["links"] + 1)
            v.tensor_tensor(beta[:, :], beta[:, :], betas[:, 2:3], ALU.subtract).then_inc(coef_ready, 1)
            dve.wait_ge(tgate_ready, 1)
            v.tensor_scalar(bv1[:, :], bv1[:, :], tgate[:, 1:2], None, ALU.mult).then_inc(chain, 1)
            dve.wait_ge(chain, PROLOGUE.count["links"] + 2)
            both(lambda j, plan: run(plan, j), dve)


def kernel(**inputs):
    import numpy as np
    import concourse.bacc as bacc
    from concourse import mybir as mb
    from concourse.bass_utils import run_bass_kernel_spmd as run

    a = {k: np.asarray(v) for k, v in inputs.items()}

    def col(*names):
        return np.stack([a[n].reshape(DIM) for n in names], 1)

    def row(v):
        return np.broadcast_to(v.reshape(1, -1), (PART, v.size))

    def chunked(v):
        return np.moveaxis(v.reshape(v.shape[:-1] + (HC, PART)), -1, 0)

    kpad = np.zeros((HEADS, HD, CTX), np.float16)
    kpad[:, 0:2] = MAX_SCALE
    io = {
        "x": a["x"], "side": a["fside_BxSxS2_0"], "ctxT": a["ctx_1024"].transpose(0, 2, 1),
        "kpad": kpad, "qpad": np.zeros((HEADS, HD, SEQ), np.float16),
    }
    flat = {
        "ident": np.eye(PART, dtype=np.float32), "iota": row(np.arange(EXPERTS, dtype=np.float32)),
        "wk0": a["L0_xattn_Wk"], "wq0": a["L0_xattn_Wq"], "wo0": a["L0_xattn_Wo"],
        "wk1": a["L1_xattn_Wk"].T, "wq1": a["L1_xattn_Wq"].T,
        "wv": np.concatenate([a["L0_xattn_Wv"], a["L1_xattn_Wv"].T], 1),
        "bcol": col("L0_xattn_bq", "L0_xattn_bk", "L1_xattn_bq", "L1_xattn_bk", "L0_xattn_bv"),
        "bv1": row(a["L1_xattn_bv"]), "bo": row(a["L0_xattn_bo"]),
        "gates": row(np.concatenate([a["g_xattn"], a["g_ffn"]])),
        "betas": row(np.stack([a[f"L1_xattn_beta_{n}"].reshape(()) for n in ("risk", "prio", "impl")])),
        "rb1": chunked(a["L0_ffn_rb1"]), "rb2": row(a["L0_ffn_rb2"]),
        "b1_0": chunked(a["L0_ffn_b1"]).reshape(PART, -1), "b1_1": chunked(a["L1_ffn_b1"]).reshape(PART, -1),
    }
    for name, pack in (("first", FIRST), ("rest", REST)):
        io[name] = np.concatenate([flat[n] for n in pack], 1)
    io["w_split0"] = np.concatenate([w for n in ("L0_ffn_w1", "L1_ffn_W1") for w in a[n]]
                                    + [a["L0_ffn_rw1"], a["L1_ffn_w_gate"].T], 1)
    io["w_split1"] = np.concatenate([w.reshape(-1, HC, PART, n).transpose(2, 0, 1, 3).reshape(PART, -1) for w, n in (
        (a["L0_ffn_w2"], DIM), (a["L1_ffn_W2"], DIM), (a["L0_ffn_rw2"], EXPERTS))], 1)
    for l in range(2):
        io[f"b2_{l}"] = a[f"L{l}_ffn_b2"]

    nc = bacc.Bacc("TRN2", target_bir_lowering=False, num_devices=1)
    arrays, aps = {}, {}
    for name, v in io.items():
        v = np.ascontiguousarray(v)
        arrays[f"in_{name}"] = v
        aps[name] = nc.dram_tensor(f"in_{name}", v.shape, mb.dt.from_np(v.dtype), kind="ExternalInput").ap()
    out = nc.dram_tensor("out_0", (BATCH, SEQ, DIM), mb.dt.float32, kind="ExternalOutput").ap()
    flamingo(nc, aps, out)
    r = run(nc, [arrays], core_ids=[0])
    return r.results[0]["out_0"]
```
